# Optimizing a Trainium2 kernel written in Bass

```python
import numpy as np
import jax
import jax.numpy as jnp

def _softmax(x, axis=-1):
    return jax.nn.softmax(x, axis=axis)

def _gelu(x):
    return jax.nn.gelu(x, approximate=True)

def _silu(x):
    return jax.nn.silu(x)

def _sigmoid(x):
    return jax.nn.sigmoid(x)

def _layernorm(x, axis=-1, eps=1e-05):
    m = jnp.mean(x, axis=axis, keepdims=True)
    v = jnp.var(x, axis=axis, keepdims=True)
    return (x - m) / jnp.sqrt(v + eps)

def _scatter_add(tgt, idx, src, axis=0):
    return tgt.at[idx].add(src)

def _segment_sum(src, seg, n):
    return jax.ops.segment_sum(src, seg, n)
kernel_name = 'mk_adj_resnorm_d4_adj_r2_753fb7'

def setup_inputs(seed: int=0):
    np.random.seed(seed)
    _w = jnp.asarray

    def _rec_inputs():
        import jax
        import jax.numpy as jnp
        _gk = jax.random.key(seed)
        x = -0.0003929 + 0.9999 * jax.random.normal(jax.random.fold_in(_gk, 1), (64, 128, 256), jnp.float32)
        _a = jax.random.bernoulli(jax.random.fold_in(_gk, 2), 0.015625, (128, 128))
        _a = jnp.logical_or(_a, jnp.eye(128, dtype=bool))
        _af = _a.astype(jnp.float32)
        _af = _af * jax.random.uniform(jax.random.fold_in(_gk, 3), (128, 128), jnp.float32, 0.05, 1)
        adj = _af
        return (x, adj)
    x, adj = _rec_inputs()

    def _L0_gnn_setup():
        import jax, jax.numpy as jnp
        import numpy as np
        B, N, D, O = (8, 2048, 256, 256)
        key = jax.random.key(seed)
        k1, k2, k3, k4 = jax.random.split(key, 4)
        x = jax.random.normal(k1, (B, N, D), dtype=jnp.float32)
        adj = jax.random.uniform(k2, (N, N), dtype=jnp.float32)
        weight = jax.random.normal(k3, (D, O), dtype=jnp.float32) * 0.02
        bias = jax.random.normal(k4, (O,), dtype=jnp.float32) * 0.02
        return {'x': x, 'adj': adj, 'weight': weight, 'bias': bias}
    _L0_gnn_all = _L0_gnn_setup()
    _L0_gnn_in = {k: v for k, v in _L0_gnn_all.items() if k in ('weight', 'bias')}
    del _L0_gnn_all

    def _L1_gnn_setup():
        import jax, jax.numpy as jnp
        import numpy as np
        ALPHA = 0.2
        key = jax.random.key(seed)
        k0, k1, k2, k3 = jax.random.split(key, 4)
        B, N, C, F = (64, 512, 256, 256)
        x = jax.random.normal(k0, (B, N, C), dtype=jnp.float32)
        W = jax.random.normal(k1, (C, F), dtype=jnp.float32) * (1.414 / np.sqrt(C + F))
        a = jax.random.normal(k2, (2 * F, 1), dtype=jnp.float32) * (1.414 / np.sqrt(2 * F + 1))
        beta = jnp.ones((1,), dtype=jnp.float32)
        mask = (jax.random.uniform(k3, (N, N)) < 0.3).astype(jnp.float32)
        return {'x': x, 'W': W, 'a': a, 'beta': beta, 'mask': mask}
    _L1_gnn_all = _L1_gnn_setup()
    _L1_gnn_in = {k: v for k, v in _L1_gnn_all.items() if k in ('W', 'a', 'beta')}
    del _L1_gnn_all

    def _L2_gnn_setup():
        import jax, jax.numpy as jnp
        import numpy as np
        B, N, D, H = (16, 1025, 256, 8)
        LN_EPS = 1e-05

        def _make_mask(key, n):
            n_proto = n - 1
            adj = jax.random.bernoulli(key, 0.03, (n_proto, n_proto)).astype(jnp.float32)
            adj = jnp.clip(adj + adj.T + jnp.eye(n_proto, dtype=jnp.float32), 0.0, 1.0)
            mask = jnp.zeros((n, n), dtype=jnp.float32)
            mask = mask.at[0, :].set(1.0).at[:, 0].set(1.0)
            mask = mask.at[1:, 1:].set(adj)
            return mask
        key = jax.random.key(seed)
        ks = jax.random.split(key, 7)
        s = 1.0 / np.sqrt(D)
        return {'x': jax.random.normal(ks[0], (B, N, D), dtype=jnp.float32), 'w_qkv': jax.random.uniform(ks[1], (D, 3 * D), dtype=jnp.float32, minval=-s, maxval=s), 'w_proj': jax.random.uniform(ks[2], (D, D), dtype=jnp.float32, minval=-s, maxval=s), 'b_proj': jnp.zeros((D,), dtype=jnp.float32), 'ln_gamma': jnp.ones((D,), dtype=jnp.float32), 'ln_beta': jnp.zeros((D,), dtype=jnp.float32), 'attn_mask': _make_mask(ks[3], N)}
    _L2_gnn_all = _L2_gnn_setup()
    _L2_gnn_in = {k: v for k, v in _L2_gnn_all.items() if k in ('w_qkv', 'w_proj', 'b_proj', 'ln_gamma', 'ln_beta')}
    del _L2_gnn_all

    def _L3_gnn_setup():
        import jax, jax.numpy as jnp
        import numpy as np
        B, N, D, T = (64, 128, 256, 3)

        def _lin(v, W, b):
            return jnp.einsum('...i,oi->...o', v, W) + b
        key = jax.random.key(seed)
        ks = jax.random.split(key, 12)
        s2 = 1.0 / np.sqrt(2 * D)
        s1 = 1.0 / np.sqrt(D)
        return {'x': jax.random.normal(ks[0], (B, N, D), jnp.float32), 'in_mat': jax.random.uniform(ks[1], (N, N), jnp.float32) / N, 'out_mat': jax.random.uniform(ks[2], (N, N), jnp.float32) / N, 'w3_w': jax.random.normal(ks[3], (D, 2 * D), jnp.float32) * s2, 'w3_b': jnp.zeros((D,), jnp.float32), 'u3_w': jax.random.normal(ks[4], (D, D), jnp.float32) * s1, 'u3_b': jnp.zeros((D,), jnp.float32), 'w4_w': jax.random.normal(ks[5], (D, 2 * D), jnp.float32) * s2, 'w4_b': jnp.zeros((D,), jnp.float32), 'w5_w': jax.random.normal(ks[6], (D, 2 * D), jnp.float32) * s2, 'w5_b': jnp.zeros((D,), jnp.float32), 'u5_w': jax.random.normal(ks[7], (D, D), jnp.float32) * s1, 'u5_b': jnp.zeros((D,), jnp.float32)}
    _L3_gnn_all = _L3_gnn_setup()
    _L3_gnn_in = {k: v for k, v in _L3_gnn_all.items() if k in ('w3_w', 'w3_b', 'u3_w', 'u3_b', 'w4_w', 'w4_b', 'w5_w', 'w5_b', 'u5_w', 'u5_b')}
    del _L3_gnn_all
    return {'x': x, 'adj': adj, 'L0_gnn_weight': _L0_gnn_in['weight'], 'L0_gnn_bias': _L0_gnn_in['bias'], 'L1_gnn_W': _L1_gnn_in['W'], 'L1_gnn_a': _L1_gnn_in['a'], 'L1_gnn_beta': _L1_gnn_in['beta'], 'L2_gnn_w_qkv': _L2_gnn_in['w_qkv'], 'L2_gnn_w_proj': _L2_gnn_in['w_proj'], 'L2_gnn_b_proj': _L2_gnn_in['b_proj'], 'L2_gnn_ln_gamma': _L2_gnn_in['ln_gamma'], 'L2_gnn_ln_beta': _L2_gnn_in['ln_beta'], 'L3_gnn_w3_w': _L3_gnn_in['w3_w'], 'L3_gnn_w3_b': _L3_gnn_in['w3_b'], 'L3_gnn_u3_w': _L3_gnn_in['u3_w'], 'L3_gnn_u3_b': _L3_gnn_in['u3_b'], 'L3_gnn_w4_w': _L3_gnn_in['w4_w'], 'L3_gnn_w4_b': _L3_gnn_in['w4_b'], 'L3_gnn_w5_w': _L3_gnn_in['w5_w'], 'L3_gnn_w5_b': _L3_gnn_in['w5_b'], 'L3_gnn_u5_w': _L3_gnn_in['u5_w'], 'L3_gnn_u5_b': _L3_gnn_in['u5_b']}

def reference(x, adj, L0_gnn_weight, L0_gnn_bias, L1_gnn_W, L1_gnn_a, L1_gnn_beta, L2_gnn_w_qkv, L2_gnn_w_proj, L2_gnn_b_proj, L2_gnn_ln_gamma, L2_gnn_ln_beta, L3_gnn_w3_w, L3_gnn_w3_b, L3_gnn_u3_w, L3_gnn_u3_b, L3_gnn_w4_w, L3_gnn_w4_b, L3_gnn_w5_w, L3_gnn_w5_b, L3_gnn_u5_w, L3_gnn_u5_b):
    import jax
    import jax.numpy as jnp

    def _L0_gnn_ref(x, adj, weight, bias):
        import jax, jax.numpy as jnp
        import numpy as np
        B, N, D, O = (8, 2048, 256, 256)
        y = jnp.einsum('nm,bmd->bnd', adj, x)
        out = jnp.einsum('bnd,do->bno', y, weight) + bias
        return out

    def _L1_gnn_ref(x, W, a, beta, mask):
        import jax, jax.numpy as jnp
        import numpy as np
        ALPHA = 0.2
        F_ = W.shape[1]
        h = jnp.einsum('bnc,cf->bnf', x, W)
        a1, a2 = (a[:F_, 0], a[F_:, 0])
        s1 = jnp.einsum('bnf,f->bn', h, a1)
        s2 = jnp.einsum('bnf,f->bn', h, a2)
        e = jax.nn.leaky_relu(s1[:, :, None] + s2[:, None, :], negative_slope=ALPHA)
        e = e * mask[None, :, :]
        att = jax.nn.softmax(e, axis=2)
        h_prime = jnp.einsum('bij,bjf->bif', att, h)
        return jax.nn.elu(h_prime + beta * h)

    def _L2_gnn_ref(x, w_qkv, w_proj, b_proj, ln_gamma, ln_beta, attn_mask):
        import jax, jax.numpy as jnp
        import numpy as np
        B, N, D, H = (16, 1025, 256, 8)
        LN_EPS = 1e-05

        def _make_mask(key, n):
            n_proto = n - 1
            adj = jax.random.bernoulli(key, 0.03, (n_proto, n_proto)).astype(jnp.float32)
            adj = jnp.clip(adj + adj.T + jnp.eye(n_proto, dtype=jnp.float32), 0.0, 1.0)
            mask = jnp.zeros((n, n), dtype=jnp.float32)
            mask = mask.at[0, :].set(1.0).at[:, 0].set(1.0)
            mask = mask.at[1:, 1:].set(adj)
            return mask
        b, n, d = x.shape
        hd = d // H
        scale = hd ** (-0.5)
        qkv = (x @ w_qkv).reshape(b, n, 3, H, hd).transpose(2, 0, 3, 1, 4)
        q, k, v = (qkv[0], qkv[1], qkv[2])
        attn = jnp.einsum('bhnd,bhmd->bhnm', q, k) * scale
        attn = jnp.where(attn_mask[None, None] == 0, -jnp.inf, attn)
        attn = jax.nn.softmax(attn, axis=-1)
        o = jnp.einsum('bhnm,bhmd->bhnd', attn, v).transpose(0, 2, 1, 3).reshape(b, n, d)
        o = o @ w_proj + b_proj
        mu = jnp.mean(o, axis=-1, keepdims=True)
        var = jnp.mean(jnp.square(o - mu), axis=-1, keepdims=True)
        ln = (o - mu) * jax.lax.rsqrt(var + LN_EPS) * ln_gamma + ln_beta
        return o + ln

    def _L3_gnn_ref(x, in_mat, out_mat, w3_w, w3_b, u3_w, u3_b, w4_w, w4_b, w5_w, w5_b, u5_w, u5_b):
        import jax, jax.numpy as jnp
        import numpy as np
        B, N, D, T = (64, 128, 256, 3)

        def _lin(v, W, b):
            return jnp.einsum('...i,oi->...o', v, W) + b
        h = x
        for _ in range(T):
            a_in = jnp.einsum('nm,bmd->bnd', in_mat, h)
            a_out = jnp.einsum('nm,bmd->bnd', out_mat, h)
            av = jnp.concatenate([a_in, a_out], axis=-1)
            z = jax.nn.sigmoid(_lin(av, w3_w, w3_b) + _lin(h, u3_w, u3_b))
            r = jax.nn.sigmoid(_lin(av, w4_w, w4_b) + _lin(h, u3_w, u3_b))
            hv = jnp.tanh(_lin(av, w5_w, w5_b) + _lin(r * h, u5_w, u5_b))
            h = (1.0 - z) * h + z * hv
        return h
    x = _layernorm(x + _L0_gnn_ref(x, adj, L0_gnn_weight, L0_gnn_bias), axis=-1)
    x = _layernorm(x + _L1_gnn_ref(x, L1_gnn_W, L1_gnn_a, L1_gnn_beta, adj), axis=-1)
    x = _layernorm(x + _L2_gnn_ref(x, L2_gnn_w_qkv, L2_gnn_w_proj, L2_gnn_b_proj, L2_gnn_ln_gamma, L2_gnn_ln_beta, adj), axis=-1)
    x = _layernorm(x + _L3_gnn_ref(x, adj, adj, L3_gnn_w3_w, L3_gnn_w3_b, L3_gnn_u3_w, L3_gnn_u3_b, L3_gnn_w4_w, L3_gnn_w4_b, L3_gnn_w5_w, L3_gnn_w5_b, L3_gnn_u5_w, L3_gnn_u5_b), axis=-1)
    return x

_drawn_inputs = setup_inputs


def setup_inputs(seed=0):
    import zlib

    import numpy as np

    out = dict(_drawn_inputs(seed))
    spreads = {'L2_gnn_b_proj': (0.0, 0.1),
     'L2_gnn_ln_gamma': (1.0, 0.2),
     'L2_gnn_ln_beta': (0.0, 0.1),
     'L3_gnn_w3_b': (0.0, 0.335),
     'L3_gnn_u3_b': (0.0, 0.32),
     'L3_gnn_w4_b': (0.0, 0.8),
     'L3_gnn_w5_b': (0.0, 0.1),
     'L3_gnn_u5_b': (0.0, 0.1)}
    factors = {'L1_gnn_a': 3.672}
    for name, (base, spread) in spreads.items():
        noise = np.random.default_rng([zlib.crc32(name.encode()), seed]).standard_normal(out[name].shape)
        drawn = base * np.exp(spread * noise) if base else spread * noise
        out[name] = jnp.asarray(drawn.astype(out[name].dtype))
    for name, factor in factors.items():
        out[name] = (out[name] * factor).astype(out[name].dtype)
    return out
```

```python
import concourse.bass as bass
from concourse import mybir
from contextlib import ExitStack

B, N, D = 64, 128, 256
G = 4
NG = B // G
KB = D // 128
H = 8
HD = D // H
HB = 128 // HD
T = 3
COLS = G * N
SCALE = float(HD) ** -0.5
SLOPE = 0.2
EPS = 1e-5
MASKED = -1e30
LOWEST = -3e38

FRONT_LNS = 4

ORDER = [
    ("a", 0), "f_adjx", ("hu", 0), ("r", 0), "f_out0", ("z", 0), ("v", 0), "f_x1t", "f_h", ("t", 0),
    ("a", 1), "f_s2", ("hu", 1), "f_attt", ("r", 1), ("z", 1), "f_hp", ("v", 1), "f_x2t", "f_k", ("t", 1),
    "f_v", "f_q",
    ("a", 2), ("f_score", 0), ("f_score", 1), ("hu", 2), ("f_turn", 0), ("r", 2), ("f_mix", 0), ("f_score", 2),
    ("f_turn", 1), ("f_mix", 1), ("f_score", 3), ("z", 2), ("f_turn", 2), ("f_mix", 2), ("v", 2),
    ("f_turn", 3), ("f_mix", 3), "f_proj", ("t", 2), "f_x3", "f_x3t",
]


def gnn_stack(nc, x, adj, adj_t, w0, b0, w1, a_vec, beta, wqkv, wp, bp, gamma, lbeta,
              w3, w4, w5, u3, u5, gate_bias, out):
    F32, F32R = mybir.dt.float32, mybir.dt.float32r
    ALU, ACT, AX = mybir.AluOpType, mybir.ActivationFunctionType, mybir.AxisListType

    ctx = ExitStack()
    with ctx:
        def sb(name, shape, dt=F32):
            return ctx.enter_context(nc.sbuf_tensor(name, shape, dt))

        def sem(name):
            return ctx.enter_context(nc.semaphore(name))

        def pair(name, shape):
            return sb(name + "_hi", shape, F32R), sb(name + "_lo", shape, F32R)

        W0, WQ, WK, WV, WP = (pair(n, [128, KB, D]) for n in ("w0", "wq", "wk", "wv", "wp"))
        W3, W4, W5, U3, U5 = (pair(n, [128, KB, D]) for n in ("w3", "w4", "w5", "u3", "u5"))
        W1 = pair("w1", [128, KB, D + 2])
        WA2 = pair("wa2", [128, KB, 128])
        adj_s = sb("adj_s", [128, N])
        adjt_s = sb("adjt_s", [128, N])
        mask = sb("mask", [128, N])
        ident = sb("ident", [128, 128])
        b0_s, bp_s, gamma_s, lbeta_s = (sb(n, [128, D]) for n in ("b0_s", "bp_s", "gamma_s", "lbeta_s"))
        beta_s = sb("beta_s", [128, 1])
        gb = sb("gb", [128, 6, KB])
        bias_r, bias_z, bias_v = (sb(n, [128, KB]) for n in ("bias_r", "bias_z", "bias_v"))
        minus_half = sb("minus_half", [128, G])
        eps = sb("eps", [128, G])
        unused = sb("unused", [128, 4])
        wa = sb("wa", [128, KB, 2])

        xin = sb("xin", [128, G, D])
        x1 = sb("x1", [128, G, D])
        fhi, flo = pair("f", [128, KB, G, N])
        hs = sb("hs", [128, G, D])
        hb = sb("hb", [128, G, D])
        s1 = sb("s1", [128, G])
        el = sb("el", [128, G, D])
        mn = sb("mn", [128, G, D])
        e_s = mn[:, 0:2, :].rearrange("p a (b n) -> p (a b) n", b=2)
        et_s = mn[:, 2:4, :].rearrange("p a (b n) -> p (a b) n", b=2)
        emax = sb("emax", [128, G])
        enm = sb("enm", [128, G])
        eden = sb("eden", [128, G])
        erd = sb("erd", [128, G])
        x2 = sb("x2", [128, G, D])
        khi, klo = pair("k", [128, KB, G, N])
        kd_hi, kd_lo = pair("kd", [128, KB, HB, G, N])
        vs = sb("vs", [128, G, D])
        P = [sb(f"p{i}", [128, H, N]) for i in range(2)]
        PT = [sb(f"pt{i}", [128, H, N]) for i in range(2)]
        pmax, pnm, pden, prd = ([sb(f"{n}{i}", [128, H]) for i in range(2)] for n in ("pmax", "pnm", "pden", "prd"))
        bst, bmv, bve, brs = sb("bst", [128, G, 6]), sb("bmv", [128, G, 2]), sb("bve", [128, G]), sb("brs", [128, G])
        x3 = sb("x3", [128, G, D])

        ht = sb("ht", [128, KB, G, N])
        hhi, hlo = pair("h", [128, KB, G, N])
        ahi, alo = pair("a", [128, KB, G, N])
        hu = sb("hu", [128, KB, G, N])
        rt = sb("rt", [128, KB, G, N])
        zt = sb("zt", [128, KB, G, N])
        rhi, rlo = pair("r", [128, KB, G, N])
        hv = sb("hv", [128, KB, G, N])
        res = hv[:, :, :, :].rearrange("p k g n -> p (k g n)").rearrange("p (g d) -> p g d", g=G)
        hn = sb("hn", [128, G, D])
        cst, cmv, cve, crs = sb("cst", [128, G, 6]), sb("cmv", [128, G, 2]), sb("cve", [128, G]), sb("crs", [128, G])

        FA, FB, LA, LB = (ctx.enter_context(nc.psum_tensor(n, [128, 2, 512], F32)) for n in ("FA", "FB", "LA", "LB"))

        def feat(ps):
            return ps[:, :, :].rearrange("p k (g n) -> p k g n", g=G)

        def node(ps):
            return ps[:, :, :].rearrange("p a (b d) -> p (a b) d", b=2)

        def heads(ps):
            return ps[:, :, :].rearrange("p a (h n) -> p (a h) n", h=HB)

        names_loads = ["ld_const", "ld_w"]
        ld_const, ld_w = (sem(n) for n in names_loads)
        setup_v, setup_g, setup_k, setup_d = (sem(n) for n in ("setup_v", "setup_g", "setup_k", "setup_d"))
        x_loaded = sem("x_loaded")
        y_mm, y_hi, y_lo = sem("y_mm"), sem("y_hi"), sem("y_lo")
        xb_done, out0_mm, x1p = sem("xb_done"), sem("out0_mm"), sem("x1p")
        ln_bn, ln_stats, ln_ve, ln_rstd, ln_done = (sem(n) for n in ("ln_bn", "ln_stats", "ln_ve", "ln_rstd", "ln_done"))
        x1t_mm, x1_hi, x1_lo = sem("x1t_mm"), sem("x1_hi"), sem("x1_lo")
        h_mm, h_copied, hb_done = sem("h_mm"), sem("h_copied"), sem("hb_done")
        s2_mm, e_sum, e_leaky, e_max, e_nm = (sem(n) for n in ("s2_mm", "e_sum", "e_leaky", "e_max", "e_nm"))
        e_exp, e_rden, e_norm = sem("e_exp"), sem("e_rden"), sem("e_norm")
        et_mm, et_copied, hp_mm = sem("et_mm"), sem("et_copied"), sem("hp_mm")
        el_sum, el_min, el_exp, el_pos, x2p = (sem(n) for n in ("el_sum", "el_min", "el_exp", "el_pos", "x2p"))
        x2t_mm, x2_hi, x2_lo = sem("x2t_mm"), sem("x2_hi"), sem("x2_lo")
        k_mm, k_hi, k_lo, k_spread = sem("k_mm"), sem("k_hi"), sem("k_lo"), sem("k_spread")
        v_mm, v_copied = sem("v_mm"), sem("v_copied")
        q_mm, q_hi, q_lo = sem("q_mm"), sem("q_hi"), sem("q_lo")
        sc_mm, sc_max, sc_nm, sc_exp, sc_rden, sc_norm = (sem(n) for n in ("sc_mm", "sc_max", "sc_nm", "sc_exp", "sc_rden", "sc_norm"))
        pt_mm, pt_copied, o_mm, o_hi, o_lo = (sem(n) for n in ("pt_mm", "pt_copied", "o_mm", "o_hi", "o_lo"))
        proj_mm, o_biased, x2b_done, on_scaled, res_sum, x3p = (sem(n) for n in ("proj_mm", "o_biased", "x2b_done", "on_scaled", "res_sum", "x3p"))
        x3t_mm, ht_set, h0_hi, h0_lo = sem("x3t_mm"), sem("ht_set"), sem("h0_hi"), sem("h0_lo")
        a_mm, a_hi, a_lo = sem("a_mm"), sem("a_hi"), sem("a_lo")
        hu_mm, hu_copied = sem("hu_mm"), sem("hu_copied")
        r_mm, r_sum, r_tanh, rh_done, rh_hi, rh_lo = (sem(n) for n in ("r_mm", "r_sum", "r_tanh", "rh_done", "rh_hi", "rh_lo"))
        z_mm, z_sum, z_tanh = sem("z_mm"), sem("z_sum"), sem("z_tanh")
        v5_mm, hv_tanh, hv_diff, hv_scaled, h_new = (sem(n) for n in ("v5_mm", "hv_tanh", "hv_diff", "hv_scaled", "h_new"))
        hs_hi, hs_lo = sem("hs_hi"), sem("hs_lo")
        hn_mm, hn_copied = sem("hn_mm"), sem("hn_copied")
        res_done, c_bn, c_stats, c_ve, c_rstd, c_done = (sem(n) for n in ("res_done", "c_bn", "c_stats", "c_ve", "c_rstd", "c_done"))
        stored = sem("stored")

        block = ctx.enter_context(nc.Block())

        def later(g):
            return not (isinstance(g, int) and g == 0)

        def three(pe, dst, lhs, rhs, start, stop):
            pe.matmul(dst, lhs[0], rhs[1], start=start, stop=False)
            pe.matmul(dst, lhs[1], rhs[0], start=False, stop=False)
            return pe.matmul(dst, lhs[0], rhs[0], start=False, stop=stop)

        def run(parts, iterate):
            def part(p, g):
                name, k = (p, None) if isinstance(p, str) else p
                f = parts.get(name)
                if f is None:
                    return
                own = g + 1 if name.startswith("f_") else g
                f(own) if k is None else f(own, k)

            for p in ORDER:
                if (p if isinstance(p, str) else p[0]).startswith("f_"):
                    part(p, -1)
            for p in ORDER:
                part(p, 0)
            with iterate(1, NG - 1) as g:
                for p in ORDER:
                    part(p, g)
            for p in ORDER:
                if not (p if isinstance(p, str) else p[0]).startswith("f_"):
                    part(p, NG - 1)

        def raw(tile, half):
            flat = tile[:, :, :] if len(tile.shape) == 3 else tile[:, :, :, :].rearrange("p k g n -> p (k g) n")
            flat = flat.rearrange("p a b -> p (a b)")
            return flat[:, half * 512:half * 512 + 512].rearrange("p (k n) -> p k n", k=KB)

        raw_w0, raw_w1 = raw(P[0], 0), raw(P[0], 1)
        raw_q, raw_k = raw(P[1], 0), raw(P[1], 1)
        raw_v, raw_p = raw(PT[0], 0), raw(PT[0], 1)
        raw_3 = [raw(PT[1], 0), raw(PT[1], 1)]
        raw_4 = [raw(hu, 0), raw(hu, 1)]
        raw_5 = [raw(rt, 0), raw(rt, 1)]
        raw_u3, raw_u5 = raw(zt, 0), raw(zt, 1)
        a_row = raw(vs, 0)
        N_CONST, N_W = 14, 14

        @block.sync
        def _(sp):
            def blocks(w):
                return w.rearrange("(k p) n -> p k n", p=128)

            def to_all(v):
                return v.rearrange("(o n) -> o n", o=1).to_broadcast((128, v.shape[0]))

            sp.dma_start(adjt_s[:, :], adj_t).then_inc(ld_const, 16)
            sp.dma_start(xin[:, :, :], x[0:G].rearrange("g n d -> n g d")).then_inc(x_loaded, 16)
            sp.dma_start(raw_w0, blocks(w0)).then_inc(ld_w, 16)
            sp.dma_start(raw_w1, blocks(w1)).then_inc(ld_w, 16)
            for t in range(2):
                sp.dma_start(a_row[:, t, :], to_all(a_vec[t])).then_inc(ld_const, 16)
            sp.dma_start(adj_s[:, :], adj).then_inc(ld_const, 16)
            sp.dma_start(b0_s[:, :], to_all(b0)).then_inc(ld_const, 16)
            sp.dma_start(beta_s[:, :], to_all(beta)).then_inc(ld_const, 16)
            sp.dma_start(bp_s[:, :], to_all(bp)).then_inc(ld_const, 16)
            sp.dma_start(gamma_s[:, :], to_all(gamma)).then_inc(ld_const, 16)
            sp.dma_start(lbeta_s[:, :], to_all(lbeta)).then_inc(ld_const, 16)
            for n in range(5):
                sp.dma_start(gb[:, n, :], gate_bias[n]).then_inc(ld_const, 16)
            for t, dst in enumerate((raw_q, raw_k, raw_v)):
                sp.dma_start(dst, blocks(wqkv[:, t * D:(t + 1) * D])).then_inc(ld_w, 16)
            sp.dma_start(raw_p, blocks(wp)).then_inc(ld_w, 16)
            for w, dst in ((w3, raw_3), (w4, raw_4), (w5, raw_5)):
                for t in range(2):
                    sp.dma_start(dst[t], blocks(w[t * D:(t + 1) * D, :])).then_inc(ld_w, 16)
            sp.dma_start(raw_u3, blocks(u3)).then_inc(ld_w, 16)
            sp.dma_start(raw_u5, blocks(u5)).then_inc(ld_w, 16)

            def load_x(g):
                if later(g):
                    sp.wait_ge(y_mm, g)
                    sp.wait_ge(xb_done, g)
                    sp.dma_start(xin[:, :, :], x[bass.ds(g * G, G)].rearrange("g n d -> n g d")).then_inc(x_loaded, 16)

            def spread_k(g):
                for half, ready, src, dst in ((0, k_hi, khi, kd_hi), (1, k_lo, klo, kd_lo)):
                    sp.wait_ge(ready, g + 1)
                    if half == 0 and later(g):
                        sp.wait_ge(sc_mm, 4 * g)
                    if half == 0 and not later(g):
                        sp.wait_ge(setup_k, 2)
                    for h in range(HB):
                        r = slice(h * HD, h * HD + HD)
                        sp.dma_start(dst[r, :, h, :, :].bitcast(F32), src[r, :, :, :].bitcast(F32)).then_inc(k_spread, 16)

            def store(g, s):
                if s == T - 1:
                    sp.wait_ge(c_done, g + 1)
                    sp.dma_start(out[bass.ds(g * G, G)].rearrange("g n d -> n g d"), res).then_inc(stored, 16)

            run({"f_adjx": load_x, "f_k": spread_k, "t": store}, sp.Fori)
            sp.wait_ge(stored, 16 * NG)

        @block.gpsimd
        def _(pool):
            pool.memset(ident[:, :], 0.0).then_inc(setup_g, 1)
            pool.wait_ge(setup_g, 1)
            pool.affine_select(out=ident[:, :], in_=ident[:, :], compare_op=ALU.not_equal, fill=1.0,
                               base=0, pattern=[[-1, 128]], channel_multiplier=1).then_inc(setup_g, 1)
            pool.memset(minus_half[:, :], -0.5).then_inc(setup_g, 1)
            pool.memset(eps[:, :], EPS).then_inc(setup_g, 1)
            pool.memset(kd_hi[:, :, :, :, :].rearrange("p k h g n -> p (k h g n)").bitcast(F32), 0.0).then_inc(setup_k, 1)
            pool.memset(kd_lo[:, :, :, :, :].rearrange("p k h g n -> p (k h g n)").bitcast(F32), 0.0).then_inc(setup_k, 1)

            def rstd(g, k):
                n = FRONT_LNS * g + k
                pool.wait_ge(ln_stats, n + 1)
                pool.tensor_tensor(bve[:, :], bmv[:, :, 1], eps[:, :], ALU.add).then_inc(ln_ve, 1)
                pool.wait_ge(ln_ve, n + 1)
                pool.tensor_tensor(brs[:, :], bve[:, :], minus_half[:, :], ALU.pow).then_inc(ln_rstd, 1)

            def adjx(g):
                if not later(g):
                    pool.wait_ge(ld_const, 16 * N_CONST)
                    pool.wait_ge(setup_g, 4)
                pool.wait_ge(x_loaded, 16 * (g + 1))
                if later(g):
                    pool.wait_ge(x2p, g)
                pool.tensor_tensor(x1[:, :, :], xin[:, :, :], b0_s[:, :].unsqueeze(1).to_broadcast((128, G, D)),
                                   ALU.add).then_inc(xb_done, 1)

            def out0(g):
                rstd(g, 0)

            def h(g):
                pool.wait_ge(h_copied, g + 1)
                pool.tensor_tensor(hb[:, :, :], hs[:, :, :], beta_s[:, 0:1].unsqueeze(2).to_broadcast((128, G, D)),
                                   ALU.mult).then_inc(hb_done, 1)

            def s2(g):
                pool.wait_ge(e_rden, g + 1)
                pool.tensor_tensor(e_s, e_s, erd[:, :].unsqueeze(2).to_broadcast((128, G, N)), ALU.mult).then_inc(e_norm, 1)

            def hp(g):
                rstd(g, 1)
                pool.wait_ge(ln_done, FRONT_LNS * g + 2)
                pool.wait_ge(hp_mm, g + 1)
                pool.tensor_tensor(hs[:, :, :], x2[:, :, :], lbeta_s[:, :].unsqueeze(1).to_broadcast((128, G, D)),
                                   ALU.add).then_inc(x2b_done, 1)

            def score(g, b):
                pool.wait_ge(sc_rden, G * g + b + 1)
                p = P[b % 2][:, :, :]
                pool.tensor_tensor(p, p, prd[b % 2][:, :].unsqueeze(2).to_broadcast((128, H, N)), ALU.mult).then_inc(sc_norm, 1)

            def proj(g):
                rstd(g, 2)
                pool.wait_ge(o_biased, g + 1)
                pool.wait_ge(x2b_done, g + 1)
                pool.tensor_tensor(hs[:, :, :], el[:, :, :], hs[:, :, :], ALU.add).then_inc(res_sum, 1)
                pool.wait_ge(ln_done, FRONT_LNS * g + 3)
                pool.tensor_tensor(mn[:, :, :], mn[:, :, :], gamma_s[:, :].unsqueeze(1).to_broadcast((128, G, D)),
                                   ALU.mult).then_inc(on_scaled, 1)

            def x3_part(g):
                rstd(g, 3)

            def last_rstd(g, s):
                if s == T - 1:
                    pool.wait_ge(c_stats, g + 1)
                    pool.tensor_tensor(cve[:, :], cmv[:, :, 1], eps[:, :], ALU.add).then_inc(c_ve, 1)
                    pool.wait_ge(c_ve, g + 1)
                    pool.tensor_tensor(crs[:, :], cve[:, :], minus_half[:, :], ALU.pow).then_inc(c_rstd, 1)

            run({"f_adjx": adjx, "f_out0": out0, "f_h": h, "f_s2": s2, "f_hp": hp, "f_score": score,
                 "f_proj": proj, "f_x3": x3_part, "t": last_rstd}, pool.Fori)

        @block.scalar
        def _(act):
            def adjx(g):
                act.wait_ge(y_mm, g + 1)
                if later(g):
                    act.wait_ge(sc_mm, 4 * g)
                act.activation(fhi[:, :, :, :], feat(FA), ACT.Copy).then_inc(y_hi, 1)

            def x1t(g):
                act.wait_ge(x1t_mm, g + 1)
                act.activation(fhi[:, :, :, :], feat(FA), ACT.Copy).then_inc(x1_hi, 1)

            def h(g):
                act.wait_ge(h_mm, g + 1)
                if later(g):
                    act.wait_ge(x3p, g)
                for i, ps in enumerate((FB, FA)):
                    act.activation(s1[:, 2 * i:2 * i + 2], ps[:, :, D], ACT.Copy)
                    last = act.activation(hs[:, 2 * i:2 * i + 2, :], ps[:, :, 0:D], ACT.Copy)
                last.then_inc(h_copied, 1)

            def s2(g):
                act.wait_ge(e_nm, g + 1)
                for b in range(G):
                    last = act.activation(e_s[:, b, :], e_s[:, b, :], ACT.Exp, bias=enm[:, b:b + 1],
                                          accum_out=eden[:, b:b + 1])
                last.then_inc(e_exp, 1)

            def attt(g):
                act.wait_ge(et_mm, g + 1)
                act.activation(et_s, FB[:, 0, :].rearrange("p (g n) -> p g n", g=G), ACT.Copy).then_inc(et_copied, 1)

            def hp(g):
                act.wait_ge(el_min, g + 1)
                act.activation(mn[:, :, :], mn[:, :, :], ACT.Exp).then_inc(el_exp, 1)

            def x2t(g):
                act.wait_ge(x2t_mm, g + 1)
                act.activation(fhi[:, :, :, :], feat(FB), ACT.Copy).then_inc(x2_hi, 1)

            def k(g):
                act.wait_ge(k_mm, g + 1)
                if later(g):
                    act.wait_ge(proj_mm, g)
                act.activation(khi[:, :, :, :], feat(FA), ACT.Copy).then_inc(k_hi, 1)

            def v(g):
                act.wait_ge(v_mm, g + 1)
                if later(g):
                    act.wait_ge(o_mm, 4 * g)
                act.activation(vs[:, :, :], node(FB), ACT.Copy).then_inc(v_copied, 1)

            def q(g):
                act.wait_ge(q_mm, g + 1)
                act.activation(fhi[:, :, :, :], feat(FA), ACT.Copy).then_inc(q_hi, 1)

            def score(g, b):
                act.wait_ge(sc_nm, G * g + b + 1)
                p = P[b % 2]
                for h_ in range(H):
                    last = act.activation(p[:, h_, :], p[:, h_, :], ACT.Exp, bias=pnm[b % 2][:, h_:h_ + 1],
                                          scale=SCALE, accum_out=pden[b % 2][:, h_:h_ + 1])
                last.then_inc(sc_exp, 1)

            def turn(g, b):
                n = G * g + b
                act.wait_ge(pt_mm, n + 1)
                if b >= 2 or later(g):
                    act.wait_ge(o_mm, n - 1)
                act.activation(PT[b % 2][:, :, :], heads((FA, FB)[b % 2]), ACT.Copy).then_inc(pt_copied, 1)

            def mix(g, b):
                act.wait_ge(o_mm, G * g + b + 1)
                if b == 0:
                    act.wait_ge(k_spread, 128 * (g + 1))
                ps = (FA, FB)[b % 2]
                act.activation(khi[:, :, b, :], ps[:, 0, 0:KB * N].rearrange("p (k n) -> p k n", k=KB),
                               ACT.Copy).then_inc(o_hi, 1)

            def x3t(g):
                act.wait_ge(x3t_mm, g + 1)
                if later(g):
                    act.wait_ge(h_new, T * g)
                    act.wait_ge(hn_mm, T * g)
                act.activation(ht[:, :, :, :], feat(FA), ACT.Copy).then_inc(ht_set, 1)
                act.activation(hhi[:, :, :, :], feat(FA), ACT.Copy).then_inc(h0_hi, 1)

            def a(g, s):
                n = T * g + s
                act.wait_ge(a_mm, n + 1)
                act.activation(ahi[:, :, :, :], feat(LA), ACT.Copy).then_inc(a_hi, 1)

            def hu_part(g, s):
                act.wait_ge(hu_mm, T * g + s + 1)
                act.activation(hu[:, :, :, :], feat(LB), ACT.Copy).then_inc(hu_copied, 1)

            def r(g, s):
                act.wait_ge(r_sum, T * g + s + 1)
                for k_ in range(KB):
                    last = act.activation(rt[:, k_, :, :], rt[:, k_, :, :], ACT.Tanh, bias=bias_r[:, k_:k_ + 1], scale=0.5)
                last.then_inc(r_tanh, 1)
                act.wait_ge(rh_done, T * g + s + 1)
                act.activation(rhi[:, :, :, :], rt[:, :, :, :], ACT.Copy).then_inc(rh_hi, 1)

            def z(g, s):
                act.wait_ge(z_sum, T * g + s + 1)
                for k_ in range(KB):
                    last = act.activation(zt[:, k_, :, :], zt[:, k_, :, :], ACT.Tanh, bias=bias_z[:, k_:k_ + 1], scale=0.5)
                last.then_inc(z_tanh, 1)

            def v5(g, s):
                act.wait_ge(v5_mm, T * g + s + 1)
                if s == 0 and later(g):
                    act.wait_ge(stored, 16 * g)
                for k_ in range(KB):
                    last = act.activation(hv[:, k_, :, :], feat(LA)[:, k_, :, :], ACT.Tanh, bias=bias_v[:, k_:k_ + 1])
                last.then_inc(hv_tanh, 1)
                if s < T - 1:
                    act.wait_ge(h_new, T * g + s + 1)
                    act.activation(hhi[:, :, :, :], ht[:, :, :, :], ACT.Copy).then_inc(hs_hi, 1)

            def t(g, s):
                if s < T - 1:
                    act.wait_ge(hn_mm, T * g + s + 1)
                    act.activation(hn[:, :, :], node(LB), ACT.Copy).then_inc(hn_copied, 1)

            act.wait_ge(setup_v, 3)
            run({"f_adjx": adjx, "f_x1t": x1t, "f_h": h, "f_s2": s2, "f_attt": attt, "f_hp": hp, "f_x2t": x2t,
                 "f_k": k, "f_v": v, "f_q": q, "f_score": score, "f_turn": turn, "f_mix": mix, "f_x3t": x3t,
                 "a": a, "hu": hu_part, "r": r, "z": z, "v": v5, "t": t}, act.Fori)

        @block.vector
        def _(dve):
            dve.wait_ge(ld_const, 16 * N_CONST)
            dve.wait_ge(ld_w, 16 * N_W)
            for dst, n1, n2, f in ((bias_z, 0, 1, 0.5), (bias_r, 2, 1, 0.5), (bias_v, 3, 4, 1.0)):
                dve.tensor_tensor(dst[:, :], gb[:, n1, :], gb[:, n2, :], ALU.add).then_inc(setup_d, 1)
            dve.wait_ge(setup_d, 3)
            for dst, f in ((bias_z, 0.5), (bias_r, 0.5), (bias_v, 1.0)):
                dve.tensor_scalar(dst[:, :], dst[:, :], f, None, ALU.mult).then_inc(setup_v, 1)
            dve.tensor_scalar(mask[:, :], adj_s[:, :], 0.0, MASKED, ALU.is_equal, ALU.mult).then_inc(setup_d, 1)
            for w in (raw_3, raw_4, raw_5):
                dve.tensor_tensor(w[0], w[0], w[1], ALU.add).then_inc(setup_d, 1)
            dve.tensor_scalar(raw_u5, raw_u5, 0.5, None, ALU.mult).then_inc(setup_d, 1)
            for k_ in range(KB):
                for t_ in range(2):
                    dve.wait_ge(setup_d, 8 + 2 * k_ + t_)
                    dve.tensor_tensor_reduce(raw(vs, 1)[:, 0, :], raw_w1[:, k_, :], a_row[:, t_, :], 1.0, 0.0, ALU.mult, ALU.add,
                                             wa[:, k_, t_:t_ + 1]).then_inc(setup_d, 1)
            dve.wait_ge(setup_d, 12)
            for w, src in ((W0, raw_w0), (WQ, raw_q), (WK, raw_k), (WV, raw_v), (WP, raw_p), (W3, raw_3[0]),
                           (W4, raw_4[0]), (W5, raw_5[0]), (U3, raw_u3), (U5, raw_u5)):
                dve.tensor_copy(w[0][:, :, :], src).then_inc(setup_d, 1)
            dve.tensor_copy(W1[0][:, :, 0:D], raw_w1).then_inc(setup_d, 1)
            dve.tensor_copy(W1[0][:, :, D:D + 2], wa[:, :, :]).then_inc(setup_d, 1)
            wa2 = wa[:, :, 1:2].to_broadcast((128, KB, 128))
            dve.tensor_copy(WA2[0][:, :, :], wa2).then_inc(setup_d, 1)
            dve.wait_ge(setup_d, 25)
            for w, src in ((W0, raw_w0), (WQ, raw_q), (WK, raw_k), (WV, raw_v), (WP, raw_p), (W3, raw_3[0]),
                           (W4, raw_4[0]), (W5, raw_5[0]), (U3, raw_u3), (U5, raw_u5)):
                dve.tensor_tensor(w[1][:, :, :], src, w[0][:, :, :], ALU.subtract).then_inc(setup_v, 1)
            dve.tensor_tensor(W1[1][:, :, 0:D], raw_w1, W1[0][:, :, 0:D], ALU.subtract).then_inc(setup_v, 1)
            dve.tensor_tensor(W1[1][:, :, D:D + 2], wa[:, :, :], W1[0][:, :, D:D + 2], ALU.subtract).then_inc(setup_v, 1)
            dve.tensor_tensor(WA2[1][:, :, :], wa2, WA2[0][:, :, :], ALU.subtract).then_inc(setup_v, 1)
            dve.wait_ge(setup_v, 16)

            def wait_apart(signal, value, spot):
                dve.wait_ge(signal, value)
                dve.memset(unused[:, spot:spot + 1], 0.0)

            def stats(g, k, src):
                n = FRONT_LNS * g + k
                for b in range(G):
                    dve.bn_stats(bst[:, b, :], src[:, b, :]).then_inc(ln_bn, 1)
                wait_apart(ln_bn, G * n + G, 0)
                for b in range(G):
                    last = dve.bn_aggr(bmv[:, b, :], bst[:, b, :])
                last.then_inc(ln_stats, 1)

            def normalise(g, k, dst, src):
                n = FRONT_LNS * g + k
                dve.wait_ge(ln_rstd, n + 1)
                for b in range(G):
                    last = dve.tensor_scalar(dst[:, b, :], src[:, b, :], bmv[:, b, 0:1], brs[:, b:b + 1],
                                             ALU.subtract, ALU.mult)
                last.then_inc(ln_done, 1)

            def adjx(g):
                dve.wait_ge(y_hi, g + 1)
                dve.tensor_tensor(flo[:, :, :, :], feat(FA), fhi[:, :, :, :], ALU.subtract).then_inc(y_lo, 1)

            def out0(g):
                dve.wait_ge(out0_mm, g + 1)
                dve.wait_ge(xb_done, g + 1)
                dve.tensor_tensor(x1[:, :, :], node(FB), x1[:, :, :], ALU.add).then_inc(x1p, 1)
                dve.wait_ge(x1p, g + 1)
                stats(g, 0, x1)
                normalise(g, 0, x1, x1)

            def x1t(g):
                dve.wait_ge(x1_hi, g + 1)
                dve.tensor_tensor(flo[:, :, :, :], feat(FA), fhi[:, :, :, :], ALU.subtract).then_inc(x1_lo, 1)

            def s2(g):
                dve.wait_ge(s2_mm, g + 1)
                dve.wait_ge(h_copied, g + 1)
                if later(g):
                    dve.wait_ge(x3p, g)
                ps = FA[:, 0, :].rearrange("p (g n) -> p g n", g=G)
                dve.tensor_tensor(e_s, ps, s1[:, :].unsqueeze(2).to_broadcast((128, G, N)), ALU.add).then_inc(e_sum, 1)
                dve.wait_ge(e_sum, g + 1)
                dve.scalar_tensor_tensor(out=e_s, in0=e_s, scalar=SLOPE, in1=e_s, op0=ALU.mult, op1=ALU.max).then_inc(e_leaky, 1)
                wait_apart(e_leaky, g + 1, 2)
                for b in range(G):
                    last = dve.tensor_tensor_reduce(e_s[:, b, :], e_s[:, b, :], adj_s[:, :], 1.0, LOWEST, ALU.mult,
                                                    ALU.max, emax[:, b:b + 1])
                last.then_inc(e_max, 1)
                dve.wait_ge(e_max, g + 1)
                dve.tensor_scalar(enm[:, :], emax[:, :], -1.0, None, ALU.mult).then_inc(e_nm, 1)
                dve.wait_ge(e_exp, g + 1)
                dve.reciprocal(erd[:, :], eden[:, :]).then_inc(e_rden, 1)

            def hp(g):
                dve.wait_ge(hp_mm, g + 1)
                dve.wait_ge(hb_done, g + 1)
                if later(g):
                    dve.wait_ge(res_sum, g)
                dve.tensor_tensor(el[:, :, :], node(FA), hb[:, :, :], ALU.add).then_inc(el_sum, 1)
                dve.wait_ge(el_sum, g + 1)
                dve.tensor_scalar(mn[:, :, :], el[:, :, :], 0.0, None, ALU.min).then_inc(el_min, 1)
                dve.wait_ge(el_exp, g + 1)
                dve.scalar_tensor_tensor(out=el[:, :, :], in0=el[:, :, :], scalar=0.0, in1=mn[:, :, :],
                                         op0=ALU.max, op1=ALU.add).then_inc(el_pos, 1)
                dve.wait_ge(el_pos, g + 1)
                dve.scalar_tensor_tensor(out=x2[:, :, :], in0=el[:, :, :], scalar=-1.0, in1=x1[:, :, :],
                                         op0=ALU.add, op1=ALU.add).then_inc(x2p, 1)
                dve.wait_ge(x2p, g + 1)
                stats(g, 1, x2)
                normalise(g, 1, x2, x2)

            def x2t(g):
                dve.wait_ge(x2_hi, g + 1)
                dve.tensor_tensor(flo[:, :, :, :], feat(FB), fhi[:, :, :, :], ALU.subtract).then_inc(x2_lo, 1)

            def k(g):
                dve.wait_ge(k_hi, g + 1)
                dve.tensor_tensor(klo[:, :, :, :], feat(FA), khi[:, :, :, :], ALU.subtract).then_inc(k_lo, 1)

            def q(g):
                dve.wait_ge(q_hi, g + 1)
                dve.tensor_tensor(flo[:, :, :, :], feat(FA), fhi[:, :, :, :], ALU.subtract).then_inc(q_lo, 1)

            def score(g, b):
                n = G * g + b
                if b >= 2 or later(g):
                    dve.wait_ge(pt_mm, n - 1)
                wait_apart(sc_mm, n + 1, 3)
                p, ps = P[b % 2], heads((FA, FB)[b % 2])
                for h_ in range(H):
                    last = dve.tensor_tensor_reduce(p[:, h_, :], ps[:, h_, :], mask[:, :], 1.0, LOWEST, ALU.add,
                                                    ALU.max, pmax[b % 2][:, h_:h_ + 1])
                last.then_inc(sc_max, 1)
                dve.wait_ge(sc_max, n + 1)
                dve.tensor_scalar(pnm[b % 2][:, :], pmax[b % 2][:, :], -SCALE, None, ALU.mult).then_inc(sc_nm, 1)
                dve.wait_ge(sc_exp, n + 1)
                dve.reciprocal(prd[b % 2][:, :], pden[b % 2][:, :]).then_inc(sc_rden, 1)

            def mix(g, b):
                dve.wait_ge(o_hi, G * g + b + 1)
                ps = (FA, FB)[b % 2][:, 0, 0:KB * N].rearrange("p (k n) -> p k n", k=KB)
                dve.tensor_tensor(klo[:, :, b, :], ps, khi[:, :, b, :], ALU.subtract).then_inc(o_lo, 1)

            def proj(g):
                dve.wait_ge(proj_mm, g + 1)
                dve.tensor_tensor(el[:, :, :], node(FA), bp_s[:, :].unsqueeze(1).to_broadcast((128, G, D)),
                                  ALU.add).then_inc(o_biased, 1)
                dve.wait_ge(o_biased, g + 1)
                stats(g, 2, el)
                normalise(g, 2, mn, el)

            def x3_part(g):
                dve.wait_ge(on_scaled, g + 1)
                dve.wait_ge(res_sum, g + 1)
                if later(g):
                    dve.wait_ge(res_done, g)
                dve.tensor_tensor(x3[:, :, :], hs[:, :, :], mn[:, :, :], ALU.add).then_inc(x3p, 1)
                dve.wait_ge(x3p, g + 1)
                stats(g, 3, x3)
                normalise(g, 3, x3, x3)

            def x3t(g):
                dve.wait_ge(h0_hi, g + 1)
                dve.tensor_tensor(hlo[:, :, :, :], ht[:, :, :, :], hhi[:, :, :, :], ALU.subtract).then_inc(h0_lo, 1)

            def a(g, s):
                dve.wait_ge(a_hi, T * g + s + 1)
                dve.tensor_tensor(alo[:, :, :, :], feat(LA), ahi[:, :, :, :], ALU.subtract).then_inc(a_lo, 1)

            def r(g, s):
                n = T * g + s
                dve.wait_ge(r_mm, n + 1)
                dve.wait_ge(hu_copied, n + 1)
                dve.tensor_tensor(rt[:, :, :, :], feat(LA), hu[:, :, :, :], ALU.add).then_inc(r_sum, 1)
                dve.wait_ge(r_tanh, n + 1)
                dve.scalar_tensor_tensor(out=rt[:, :, :, :], in0=rt[:, :, :, :], scalar=1.0, in1=ht[:, :, :, :],
                                         op0=ALU.add, op1=ALU.mult).then_inc(rh_done, 1)
                dve.wait_ge(rh_hi, n + 1)
                dve.tensor_tensor(rlo[:, :, :, :], rt[:, :, :, :], rhi[:, :, :, :], ALU.subtract).then_inc(rh_lo, 1)

            def z(g, s):
                n = T * g + s
                dve.wait_ge(z_mm, n + 1)
                dve.tensor_tensor(zt[:, :, :, :], feat(LB), hu[:, :, :, :], ALU.add).then_inc(z_sum, 1)

            def v5(g, s):
                n = T * g + s
                dve.wait_ge(hv_tanh, n + 1)
                dve.wait_ge(z_tanh, n + 1)
                dve.tensor_tensor(hv[:, :, :, :], hv[:, :, :, :], ht[:, :, :, :], ALU.subtract).then_inc(hv_diff, 1)
                dve.wait_ge(hv_diff, n + 1)
                dve.scalar_tensor_tensor(out=hv[:, :, :, :], in0=zt[:, :, :, :], scalar=1.0, in1=hv[:, :, :, :],
                                         op0=ALU.add, op1=ALU.mult).then_inc(hv_scaled, 1)
                dve.wait_ge(hv_scaled, n + 1)
                dve.scalar_tensor_tensor(out=ht[:, :, :, :], in0=hv[:, :, :, :], scalar=0.5, in1=ht[:, :, :, :],
                                         op0=ALU.mult, op1=ALU.add).then_inc(h_new, 1)
                if s < T - 1:
                    dve.wait_ge(hs_hi, (T - 1) * g + s + 1)
                    dve.tensor_tensor(hlo[:, :, :, :], ht[:, :, :, :], hhi[:, :, :, :], ALU.subtract).then_inc(hs_lo, 1)

            def t(g, s):
                if s < T - 1:
                    return
                dve.wait_ge(hn_mm, T * g + T)
                dve.tensor_tensor(res, node(LB), x3[:, :, :], ALU.add).then_inc(res_done, 1)
                dve.wait_ge(res_done, g + 1)
                for b in range(G):
                    dve.bn_stats(cst[:, b, :], res[:, b, :]).then_inc(c_bn, 1)
                wait_apart(c_bn, G * g + G, 1)
                for b in range(G):
                    last = dve.bn_aggr(cmv[:, b, :], cst[:, b, :])
                last.then_inc(c_stats, 1)
                dve.wait_ge(c_rstd, g + 1)
                for b in range(G):
                    last = dve.tensor_scalar(res[:, b, :], res[:, b, :], cmv[:, b, 0:1], crs[:, b:b + 1],
                                             ALU.subtract, ALU.mult)
                last.then_inc(c_done, 1)

            run({"f_adjx": adjx, "f_out0": out0, "f_x1t": x1t, "f_s2": s2, "f_hp": hp, "f_x2t": x2t,
                 "f_k": k, "f_q": q, "f_score": score, "f_mix": mix, "f_proj": proj, "f_x3": x3_part, "f_x3t": x3t,
                 "a": a, "r": r, "z": z, "v": v5, "t": t}, dve.Fori)

        @block.tensor
        def _(pe):
            def features(ps, w, hi, lo):
                for o in range(KB):
                    for k_ in range(KB):
                        cols = slice(o * 128, o * 128 + 128)
                        last = three(pe, ps[:, o, :], (w[0][:, k_, cols], w[1][:, k_, cols]),
                                     (flat(hi, k_), flat(lo, k_)), k_ == 0, k_ == KB - 1)
                return last

            def flat(tile, k_):
                return tile[:, k_, :, :].rearrange("p g n -> p (g n)")

            def nodes(dst, w, hi, lo, width=D):
                for b in range(G):
                    for k_ in range(KB):
                        last = three(pe, dst(b), (hi[:, k_, b, :], lo[:, k_, b, :]),
                                     (w[0][:, k_, 0:width], w[1][:, k_, 0:width]), k_ == 0, k_ == KB - 1)
                return last

            def turn_nodes(ps, src):
                for k_ in range(KB):
                    for b in range(G):
                        last = pe.transpose(feat(ps)[:, k_, b, :], src[:, b, k_ * 128:k_ * 128 + 128], ident[:, :])
                return last

            def adjx(g):
                pe.wait_ge(x_loaded, 16 * (g + 1))
                if later(g):
                    pe.wait_ge(ht_set, g)
                    pe.wait_ge(h0_hi, g)
                for k_ in range(KB):
                    for b in range(G):
                        last = pe.matmul(feat(FA)[:, k_, b, :], xin[:, b, k_ * 128:k_ * 128 + 128], adjt_s[:, :],
                                         start=True, stop=True)
                last.then_inc(y_mm, 1)

            def out0(g):
                pe.wait_ge(y_lo, g + 1)
                nodes(lambda b: node(FB)[:, b, :], W0, fhi, flo).then_inc(out0_mm, 1)

            def x1t(g):
                pe.wait_ge(ln_done, FRONT_LNS * g + 1)
                turn_nodes(FA, x1).then_inc(x1t_mm, 1)

            def h(g):
                pe.wait_ge(x1_lo, g + 1)
                nodes(lambda b: (FB, FA)[b // 2][:, b % 2, 0:D + 2], W1, fhi, flo, D + 2).then_inc(h_mm, 1)

            def s2(g):
                pe.wait_ge(h_copied, g + 1)
                for k_ in range(KB):
                    last = three(pe, FA[:, 0, :], (WA2[0][:, k_, :], WA2[1][:, k_, :]),
                                 (flat(fhi, k_), flat(flo, k_)), k_ == 0, k_ == KB - 1)
                last.then_inc(s2_mm, 1)

            def attt(g):
                pe.wait_ge(e_norm, g + 1)
                for b in range(G):
                    last = pe.transpose(FB[:, 0, b * N:b * N + N], e_s[:, b, :], ident[:, :])
                last.then_inc(et_mm, 1)

            def hp(g):
                pe.wait_ge(et_copied, g + 1)
                for b in range(G):
                    last = pe.matmul(node(FA)[:, b, :], et_s[:, b, :], hs[:, b, :], start=True, stop=True)
                last.then_inc(hp_mm, 1)

            def x2t(g):
                pe.wait_ge(ln_done, FRONT_LNS * g + 2)
                turn_nodes(FB, x2).then_inc(x2t_mm, 1)

            def k(g):
                pe.wait_ge(x2_lo, g + 1)
                features(FA, WK, fhi, flo).then_inc(k_mm, 1)

            def v(g):
                nodes(lambda b: node(FB)[:, b, :], WV, fhi, flo).then_inc(v_mm, 1)

            def q(g):
                pe.wait_ge(k_lo, g + 1)
                features(FA, WQ, fhi, flo).then_inc(q_mm, 1)

            def score(g, b):
                n = G * g + b
                ps = (FA, FB)[b % 2]
                if b == 0:
                    pe.wait_ge(q_lo, g + 1)
                    pe.wait_ge(k_spread, 128 * (g + 1))
                if b == 1:
                    pe.wait_ge(v_copied, g + 1)
                if b >= 2:
                    pe.wait_ge(o_lo, n - 1)
                for k_ in range(KB):
                    last = three(pe, ps[:, k_, :], (fhi[:, k_, b, :], flo[:, k_, b, :]),
                                 (kd_hi[:, k_, :, b, :], kd_lo[:, k_, :, b, :]), True, True)
                last.then_inc(sc_mm, 1)

            def turn(g, b):
                n = G * g + b
                pe.wait_ge(sc_norm, n + 1)
                for h_ in range(H):
                    last = pe.transpose(heads((FA, FB)[b % 2])[:, h_, :], P[b % 2][:, h_, :], ident[:, :])
                last.then_inc(pt_mm, 1)

            def mix(g, b):
                n = G * g + b
                pe.wait_ge(pt_copied, n + 1)
                for k_ in range(KB):
                    for h_ in range(HB):
                        f = k_ * 128 + h_ * HD
                        last = pe.matmul((FA, FB)[b % 2][h_ * HD:h_ * HD + HD, 0, k_ * N:k_ * N + N],
                                         vs[:, b, f:f + HD], PT[b % 2][:, k_ * HB + h_, :], start=True, stop=True)
                last.then_inc(o_mm, 1)

            def proj(g):
                pe.wait_ge(o_lo, G * g + G)
                nodes(lambda b: node(FA)[:, b, :], WP, khi, klo).then_inc(proj_mm, 1)

            def x3t(g):
                pe.wait_ge(ln_done, FRONT_LNS * g + 4)
                turn_nodes(FA, x3).then_inc(x3t_mm, 1)

            def a(g, s):
                n = T * g + s
                if s:
                    pe.wait_ge(hn_copied, (T - 1) * g + s)
                    pe.wait_ge(hv_tanh, n)
                elif later(g):
                    pe.wait_ge(hv_tanh, n)
                    pe.wait_ge(ln_done, FRONT_LNS * (g + 1))
                else:
                    pe.wait_ge(ln_done, FRONT_LNS * (g + 1))
                src = hn if s else x3
                for k_ in range(KB):
                    for b in range(G):
                        last = pe.matmul(feat(LA)[:, k_, b, :], src[:, b, k_ * 128:k_ * 128 + 128], adjt_s[:, :],
                                         start=True, stop=True)
                last.then_inc(a_mm, 1)

            def hu_part(g, s):
                if s == 0:
                    pe.wait_ge(h0_lo, g + 1)
                    if later(g):
                        pe.wait_ge(res_done, g)
                else:
                    pe.wait_ge(hs_lo, (T - 1) * g + s)
                features(LB, U3, hhi, hlo).then_inc(hu_mm, 1)

            def r(g, s):
                pe.wait_ge(a_lo, T * g + s + 1)
                features(LA, W4, ahi, alo).then_inc(r_mm, 1)

            def z(g, s):
                pe.wait_ge(hu_copied, T * g + s + 1)
                features(LB, W3, ahi, alo).then_inc(z_mm, 1)

            def v5(g, s):
                n = T * g + s
                pe.wait_ge(r_sum, n + 1)
                for w, hi, lo, first in ((W5, ahi, alo, True), (U5, rhi, rlo, False)):
                    if not first:
                        pe.wait_ge(rh_lo, n + 1)
                    for o in range(KB):
                        for k_ in range(KB):
                            cols = slice(o * 128, o * 128 + 128)
                            last = three(pe, LA[:, o, :], (w[0][:, k_, cols], w[1][:, k_, cols]),
                                         (flat(hi, k_), flat(lo, k_)), first and k_ == 0, not first and k_ == KB - 1)
                last.then_inc(v5_mm, 1)

            def t(g, s):
                n = T * g + s
                pe.wait_ge(h_new, n + 1)
                pe.wait_ge(z_sum, n + 1)
                for b in range(G):
                    for k_ in range(KB):
                        last = pe.transpose(node(LB)[:, b, k_ * 128:k_ * 128 + 128], ht[:, k_, b, :], ident[:, :])
                last.then_inc(hn_mm, 1)

            pe.wait_ge(ld_const, 16 * N_CONST)
            pe.wait_ge(setup_v, 16)
            pe.wait_ge(setup_g, 2)
            run({"f_adjx": adjx, "f_out0": out0, "f_x1t": x1t, "f_h": h, "f_s2": s2, "f_attt": attt, "f_hp": hp,
                 "f_x2t": x2t, "f_k": k, "f_v": v, "f_q": q, "f_score": score, "f_turn": turn, "f_mix": mix,
                 "f_proj": proj, "f_x3t": x3t, "a": a, "hu": hu_part, "r": r, "z": z, "v": v5, "t": t}, pe.Fori)


def kernel(**inputs):
    import numpy as _np
    import concourse.bacc as _bacc
    from concourse import mybir as _mybir
    from concourse.bass_utils import run_bass_kernel_spmd as _run

    i = {k: _np.asarray(v) for k, v in inputs.items()}

    def by_block(v):
        return v.reshape(KB, 128).T

    arrays = {
        "x": i["x"], "adj": i["adj"], "adj_t": i["adj"].T,
        "w0": i["L0_gnn_weight"], "b0": i["L0_gnn_bias"],
        "w1": i["L1_gnn_W"], "a_vec": i["L1_gnn_a"].reshape(2, D), "beta": i["L1_gnn_beta"],
        "wqkv": i["L2_gnn_w_qkv"], "wp": i["L2_gnn_w_proj"], "bp": i["L2_gnn_b_proj"],
        "gamma": i["L2_gnn_ln_gamma"], "lbeta": i["L2_gnn_ln_beta"],
        "w3": i["L3_gnn_w3_w"].T, "w4": i["L3_gnn_w4_w"].T, "w5": i["L3_gnn_w5_w"].T,
        "u3": i["L3_gnn_u3_w"].T, "u5": i["L3_gnn_u5_w"].T,
        "gate_bias": _np.stack([by_block(i[f"L3_gnn_{n}_b"]) for n in ("w3", "u3", "w4", "w5", "u5")]),
    }
    nc = _bacc.Bacc("TRN2", target_bir_lowering=False, num_devices=1)
    ins, args = {}, []
    for name, a in arrays.items():
        a = _np.ascontiguousarray(a)
        ins[f"in_{name}"] = a
        args.append(nc.dram_tensor(f"in_{name}", a.shape, _mybir.dt.from_np(a.dtype), kind="ExternalInput").ap())
    args.append(nc.dram_tensor("out", (B, N, D), _mybir.dt.float32, kind="ExternalOutput").ap())
    gnn_stack(nc, *args)
    r = _run(nc, [ins], core_ids=[0])
    return r.results[0]["out"]
```

```python
import concourse.bass as bass
from concourse import mybir
from contextlib import ExitStack

B, N, D = 64, 128, 256
G = 4
NG = B // G
KB = D // 128
H = 8
HD = D // H
HB = 128 // HD
T = 3
COLS = G * N
SCALE = float(HD) ** -0.5
SLOPE = 0.2
EPS = 1e-5
MASKED = -1e30
LOWEST = -3e38

ATT_LNS = 2

TENSOR_ORDER = """
    g_hu.0+0 g_r.0+0 g_z.0+0 m_k+1 g_v.0+0 c_x1t+2 g_u5.0+0 m_v+1 g_u5.1+0 m_q+1 g_turn.0+0 g_turn.1+0
    c_h.0+2 m_score.0+1 g_a.1+0 c_h.1+2 m_score.1+1 g_hu.1+0 g_r.1+0 c_s2+2 m_turn.0+1 g_z.1+0 m_mix.0+1
    g_v.1+0 m_score.2+1 g_u5.2+0 c_et+2 m_turn.1+1 g_u5.3+0 m_mix.1+1 c_hp+2 g_turn.2+0 m_score.3+1
    g_turn.3+0 g_a.2+0 m_turn.2+1 g_hu.2+0 m_mix.2+1 c_y+3 m_turn.3+1 g_r.2+0 m_mix.3+1 g_z.2+0 m_proj+1
    g_v.2+0 g_u5.4+0 g_u5.5+0 c_out0+3 g_turn.4+0 g_turn.5+0 m_x3t+1 g_a.0+1 m_x2t+2
"""
SCALAR_ORDER = """
    g_rtanh.2+0 c_yhi+3 g_rhi.2+0 g_ztanh.2+0 c_norm1+2 g_vtanh.4+0 m_norm0+1 g_vtanh.5+0 m_ht+1 m_h0hi+1
    g_ahi.0+1 m_x2hi+2 g_hucopy.0+1 c_norm0+3 g_norm+0 g_rtanh.0+1 g_rhi.0+1 m_khi+2 g_ztanh.0+1
    g_vtanh.0+1 c_x1hi+3 m_vcopy+2 g_vtanh.1+1 m_qhi+2 g_hhi.0+1 g_hncopy.0+1 g_hhi.1+1 c_hcopy.0+3
    g_ahi.1+1 c_hcopy.1+3 m_exp.0+2 g_hucopy.1+1 m_exp.1+2 m_ptcopy.0+2 g_rtanh.1+1 m_ohi.0+2 g_rhi.1+1
    c_exp+3 g_ztanh.1+1 c_etcopy+3 g_vtanh.2+1 m_ptcopy.1+2 g_vtanh.3+1 m_ohi.1+2 m_exp.2+2 g_hncopy.1+1
    g_hhi.3+1 g_hhi.2+1 m_exp.3+2 m_ptcopy.2+2 g_ahi.2+1 m_ohi.2+2 c_eluexp+3 g_hucopy.2+1 m_ptcopy.3+2
    m_ohi.3+2
"""
VECTOR_ORDER = """
    m_prd.3+1 m_olo.2+1 g_alo.2+0 c_eluout+2 g_rsum.2+0 m_olo.3+1 c_stats1+2 g_rh.2+0 g_zsum.2+0
    m_stats0+1 c_ylo+3 g_update.4+0 g_update.5+0 m_x3sum+1 m_stats1+1 g_res+0 m_norm1+1 c_stats0+3
    m_h0lo+1 g_alo.0+1 g_stats+0 g_rsum.0+1 m_x2lo+2 g_rh.0+1 m_klo+2 g_zsum.0+1 g_update.0+1 c_x1lo+3
    g_update.1+1 m_qlo+2 g_hlo.0+1 m_max.0+2 g_hlo.1+1 g_alo.1+1 m_max.1+2 m_prd.0+2 g_rsum.1+1 c_scores+3
    m_prd.1+2 g_rh.1+1 m_olo.0+2 g_zsum.1+1 c_erd+3 m_max.2+2 g_update.2+1 m_olo.1+2 g_update.3+1
    m_prd.2+2 m_max.3+2 g_hlo.3+1 g_hlo.2+1 c_eluin+3
"""
POOL_ORDER = """
    g_rlo.1+0 c_enorm+2 m_pnorm.2+1 m_x2b+1 m_pnorm.3+1 c_rstd.1+2 g_rlo.2+0 m_rstd.0+1 m_residual+1
    m_gamma+1 c_xb+3 m_rstd.1+1 c_rstd.0+3 g_rstd+0 g_rlo.0+1 m_pnorm.0+2 m_pnorm.1+2
"""
SYNC_ORDER = "m_spread.1+1 c_load+4 g_store+0 m_spread.0+2"
AHEAD = 4


def gnn_stack(nc, x, adj, adj_t, w0, b0, w1, a_vec, beta, wqkv, wp, bp, gamma, lbeta,
              w3, w4, w5, u3, u5, gate_bias, out):
    F32, F32R = mybir.dt.float32, mybir.dt.float32r
    ALU, ACT, AX = mybir.AluOpType, mybir.ActivationFunctionType, mybir.AxisListType

    ctx = ExitStack()
    with ctx:
        def sb(name, shape, dt=F32):
            return ctx.enter_context(nc.sbuf_tensor(name, shape, dt))

        def sem(name):
            return ctx.enter_context(nc.semaphore(name))

        def pair(name, shape):
            return sb(name + "_hi", shape, F32R), sb(name + "_lo", shape, F32R)

        W0, WQ, WK, WV, WP = (pair(n, [128, KB, D]) for n in ("w0", "wq", "wk", "wv", "wp"))
        W3, W4, W5, U3, U5 = (pair(n, [128, KB, D]) for n in ("w3", "w4", "w5", "u3", "u5"))
        W1 = pair("w1", [128, KB, D + 2])
        WA2 = pair("wa2", [128, KB, 128])
        adj_s = sb("adj_s", [128, N])
        adjt_s = sb("adjt_s", [128, N])
        mask = sb("mask", [128, N])
        ident = sb("ident", [128, 128])
        b0_s, bp_s, gamma_s, lbeta_s = (sb(n, [128, D]) for n in ("b0_s", "bp_s", "gamma_s", "lbeta_s"))
        beta_s = sb("beta_s", [128, 1])
        gb = sb("gb", [128, 6, KB])
        bias_r, bias_z, bias_v = (sb(n, [128, KB]) for n in ("bias_r", "bias_z", "bias_v"))
        minus_half = sb("minus_half", [128, G])
        minus_one = sb("minus_one", [128, G])
        eps = sb("eps", [128, G])
        unused = sb("unused", [128, 5])
        wa = sb("wa", [128, KB, 2])

        xin = sb("xin", [128, G, D])
        x1 = sb("x1", [128, G, D])
        chi, clo = pair("c", [128, KB, G, N])
        hs = sb("hs", [128, G, D])
        s1 = sb("s1", [128, G])
        el = sb("el", [128, G, D])
        mn = sb("mn", [128, G, D])
        e_s = mn[:, 0:2, :].rearrange("p a (b n) -> p (a b) n", b=2)
        et_s = mn[:, 2:4, :].rearrange("p a (b n) -> p (a b) n", b=2)
        emax, enm, eden, erd = (sb(n, [128, G]) for n in ("emax", "enm", "eden", "erd"))

        x2 = sb("x2", [128, G, D])
        x2b = sb("x2b", [128, G, D])
        fhi, flo = pair("f", [128, KB, G, N])
        khi, klo = pair("k", [128, KB, G, N])
        kd_hi, kd_lo = pair("kd", [128, KB, HB, 2, N])
        vs = sb("vs", [128, G, D])
        P = [sb(f"p{i}", [128, H, N]) for i in range(2)]
        PT = [sb(f"pt{i}", [128, H, N]) for i in range(2)]
        pmax, pnm, pden, prd = ([sb(f"{n}{i}", [128, H]) for i in range(2)] for n in ("pmax", "pnm", "pden", "prd"))
        ob = sb("ob", [128, G, D])
        on = sb("on", [128, G, D])
        x3 = sb("x3", [128, G, D])

        ht = sb("ht", [128, KB, G, N])
        hhi, hlo = pair("h", [128, KB, G, N])
        ahi, alo = pair("a", [128, KB, G, N])
        hu = sb("hu", [128, KB, G, N])
        rt = sb("rt", [128, KB, G, N])
        zt = sb("zt", [128, KB, G, N])
        rhi, rlo = pair("r", [128, KB, G, N])
        hv = sb("hv", [128, KB, G, N])
        res = hv[:, :, :, :].rearrange("p k g n -> p (k g n)").rearrange("p (g d) -> p g d", g=G)
        hn = sb("hn", [128, G, D])

        def ln_tiles(n):
            return (sb(n + "_bn", [128, G, 6]), sb(n + "_mv", [128, G, 2]), sb(n + "_ve", [128, G]),
                    sb(n + "_rs", [128, G]), sb(n + "_nm", [128, G]), sb(n + "_mr", [128, G]))

        c_ln, m_ln, g_ln = ln_tiles("cln"), ln_tiles("mln"), ln_tiles("gln")

        CP, MP, GP, GQ = (ctx.enter_context(nc.psum_tensor(n, [128, 2, 512], F32)) for n in ("CP", "MP", "GP", "GQ"))

        def feat(ps):
            return ps[:, :, :].rearrange("p k (g n) -> p k g n", g=G)

        def node(ps):
            return ps[:, :, :].rearrange("p a (b d) -> p (a b) d", b=2)

        def heads(ps):
            return ps[:, :, :].rearrange("p a (h n) -> p (a h) n", h=HB)

        ld_const, ld_w = sem("ld_const"), sem("ld_w")
        setup_v, setup_g, setup_k, setup_d = (sem(n) for n in ("setup_v", "setup_g", "setup_k", "setup_d"))
        x_loaded = sem("x_loaded")
        y_mm, y_hi, y_lo = sem("y_mm"), sem("y_hi"), sem("y_lo")
        xb_done, out0_mm, x1p = sem("xb_done"), sem("out0_mm"), sem("x1p")
        c_bn, c_stats, c_ve, c_pow, c_nm, c_rstd, c_done = (sem("c_" + n) for n in ("bn", "stats", "ve", "pow", "nm", "rstd", "done"))
        m_bn, m_stats, m_ve, m_pow, m_nm, m_rstd, m_done = (sem("m_" + n) for n in ("bn", "stats", "ve", "pow", "nm", "rstd", "done"))
        g_bn, g_stats, g_ve, g_pow, g_nm, g_rstd, g_done = (sem("g_" + n) for n in ("bn", "stats", "ve", "pow", "nm", "rstd", "done"))
        x1t_mm, x1_hi, x1_lo = sem("x1t_mm"), sem("x1_hi"), sem("x1_lo")
        h_mm, h_copied = sem("h_mm"), sem("h_copied")
        s2_mm, e_sum, e_leaky, e_max, e_nm = (sem(n) for n in ("s2_mm", "e_sum", "e_leaky", "e_max", "e_nm"))
        e_exp, e_rden, e_norm = sem("e_exp"), sem("e_rden"), sem("e_norm")
        et_mm, et_copied, hp_mm = sem("et_mm"), sem("et_copied"), sem("hp_mm")
        el_sum, el_min, el_exp, el_pos, x2p = (sem(n) for n in ("el_sum", "el_min", "el_exp", "el_pos", "x2p"))
        x2t_mm, x2_hi, x2_lo = sem("x2t_mm"), sem("x2_hi"), sem("x2_lo")
        k_mm, k_hi, k_lo, k_spread = sem("k_mm"), sem("k_hi"), sem("k_lo"), sem("k_spread")
        v_mm, v_copied = sem("v_mm"), sem("v_copied")
        q_mm, q_hi, q_lo = sem("q_mm"), sem("q_hi"), sem("q_lo")
        sc_mm, sc_max, sc_nm, sc_exp, sc_rden, sc_norm = (sem(n) for n in ("sc_mm", "sc_max", "sc_nm", "sc_exp", "sc_rden", "sc_norm"))
        pt_mm, pt_copied, o_mm, o_hi, o_lo = (sem(n) for n in ("pt_mm", "pt_copied", "o_mm", "o_hi", "o_lo"))
        proj_mm, o_biased, x2b_done, on_scaled, res_sum, x3p = (sem(n) for n in ("proj_mm", "o_biased", "x2b_done", "on_scaled", "res_sum", "x3p"))
        x3t_mm, ht_set, h0_hi, h0_lo = sem("x3t_mm"), sem("ht_set"), sem("h0_hi"), sem("h0_lo")
        a_mm, a_hi, a_lo = sem("a_mm"), sem("a_hi"), sem("a_lo")
        hu_mm, hu_copied = sem("hu_mm"), sem("hu_copied")
        r_mm, r_sum, r_tanh, rh_done, rh_hi, rh_lo = (sem(n) for n in ("r_mm", "r_sum", "r_tanh", "rh_done", "rh_hi", "rh_lo"))
        z_mm, z_sum, z_tanh = sem("z_mm"), sem("z_sum"), sem("z_tanh")
        hv_mm, hv_tanh, hv_diff, hv_scaled, h_new = (sem(n) for n in ("hv_mm", "hv_tanh", "hv_diff", "hv_scaled", "h_new"))
        h_hi, h_lo, hn_mm = sem("h_hi"), sem("h_lo"), sem("hn_mm")
        hn_copied = sem("hn_copied")
        res_done = sem("res_done")
        stored = sem("stored")

        block = ctx.enter_context(nc.Block())

        def later(g):
            return not (isinstance(g, int) and g == 0)

        def three(pe, dst, lhs, rhs, start, stop):
            pe.matmul(dst, lhs[0], rhs[1], start=start, stop=False)
            pe.matmul(dst, lhs[1], rhs[0], start=False, stop=False)
            return pe.matmul(dst, lhs[0], rhs[0], start=False, stop=stop)

        def run(order, parts, iterate):
            table = []
            for entry in order.split():
                what, ahead = entry.split("+")
                name, _, k = what.partition(".")
                table.append((parts[name], (int(k),) if k else (), int(ahead)))
            most = AHEAD

            def iteration(g):
                for part, k, ahead in table:
                    if not isinstance(g, int) or 0 <= g + ahead < NG:
                        part(g + ahead, *k)

            for g in range(-most, 1):
                iteration(g)
            with iterate(1, NG - most) as g:
                iteration(g)
            for g in range(NG - most, NG):
                iteration(g)

        def raw(tile, half):
            flat = tile[:, :, :] if len(tile.shape) == 3 else tile[:, :, :, :].rearrange("p k g n -> p (k g) n")
            flat = flat.rearrange("p a b -> p (a b)")
            return flat[:, half * 512:half * 512 + 512].rearrange("p (k n) -> p k n", k=KB)

        raw_w0, raw_w1 = raw(P[0], 0), raw(P[0], 1)
        raw_q, raw_k = raw(P[1], 0), raw(P[1], 1)
        raw_v, raw_p = raw(PT[0], 0), raw(PT[0], 1)
        raw_3 = [raw(PT[1], 0), raw(PT[1], 1)]
        raw_4 = [raw(hu, 0), raw(hu, 1)]
        raw_5 = [raw(rt, 0), raw(rt, 1)]
        raw_u3, raw_u5 = raw(zt, 0), raw(zt, 1)
        a_row = raw(vs, 0)
        N_CONST, N_W = 14, 14

        @block.sync
        def _(sp):
            def blocks(w):
                return w.rearrange("(k p) n -> p k n", p=128)

            def to_all(v):
                return v.rearrange("(o n) -> o n", o=1).to_broadcast((128, v.shape[0]))

            sp.dma_start(adjt_s[:, :], adj_t).then_inc(ld_const, 16)
            sp.dma_start(xin[:, :, :], x[0:G].rearrange("g n d -> n g d")).then_inc(x_loaded, 16)
            sp.dma_start(raw_w0, blocks(w0)).then_inc(ld_w, 16)
            sp.dma_start(raw_w1, blocks(w1)).then_inc(ld_w, 16)
            for t in range(2):
                sp.dma_start(a_row[:, t, :], to_all(a_vec[t])).then_inc(ld_const, 16)
            sp.dma_start(adj_s[:, :], adj).then_inc(ld_const, 16)
            sp.dma_start(b0_s[:, :], to_all(b0)).then_inc(ld_const, 16)
            sp.dma_start(beta_s[:, :], to_all(beta)).then_inc(ld_const, 16)
            sp.dma_start(bp_s[:, :], to_all(bp)).then_inc(ld_const, 16)
            sp.dma_start(gamma_s[:, :], to_all(gamma)).then_inc(ld_const, 16)
            sp.dma_start(lbeta_s[:, :], to_all(lbeta)).then_inc(ld_const, 16)
            for n in range(5):
                sp.dma_start(gb[:, n, :], gate_bias[n]).then_inc(ld_const, 16)
            for t, dst in enumerate((raw_q, raw_k, raw_v)):
                sp.dma_start(dst, blocks(wqkv[:, t * D:(t + 1) * D])).then_inc(ld_w, 16)
            sp.dma_start(raw_p, blocks(wp)).then_inc(ld_w, 16)
            for w, dst in ((w3, raw_3), (w4, raw_4), (w5, raw_5)):
                for t in range(2):
                    sp.dma_start(dst[t], blocks(w[t * D:(t + 1) * D, :])).then_inc(ld_w, 16)
            sp.dma_start(raw_u3, blocks(u3)).then_inc(ld_w, 16)
            sp.dma_start(raw_u5, blocks(u5)).then_inc(ld_w, 16)

            def load_x(g):
                if later(g):
                    sp.wait_ge(y_mm, g)
                    sp.wait_ge(xb_done, g)
                    sp.dma_start(xin[:, :, :], x[bass.ds(g * G, G)].rearrange("g n d -> n g d")).then_inc(x_loaded, 16)

            def spread_k(g, pair_):
                if pair_ == 0:
                    sp.wait_ge(k_lo, g + 1)
                    if later(g):
                        sp.wait_ge(sc_mm, 4 * g)
                    else:
                        sp.wait_ge(setup_k, 2)
                else:
                    sp.wait_ge(sc_mm, 4 * g + 2)
                own = slice(2 * pair_, 2 * pair_ + 2)
                for src, dst in ((khi, kd_hi), (klo, kd_lo)):
                    for h in range(HB):
                        r = slice(h * HD, h * HD + HD)
                        sp.dma_start(dst[r, :, h, :, :].bitcast(F32), src[r, :, own, :].bitcast(F32)).then_inc(k_spread, 16)

            def store(g):
                sp.wait_ge(g_done, g + 1)
                sp.dma_start(out[bass.ds(g * G, G)].rearrange("g n d -> n g d"), res).then_inc(stored, 16)

            run(SYNC_ORDER, {"c_load": load_x, "m_spread": spread_k, "g_store": store}, sp.Fori)
            sp.wait_ge(stored, 16 * NG)

        @block.gpsimd
        def _(pool):
            pool.memset(ident[:, :], 0.0).then_inc(setup_g, 1)
            pool.wait_ge(setup_g, 1)
            pool.affine_select(out=ident[:, :], in_=ident[:, :], compare_op=ALU.not_equal, fill=1.0,
                               base=0, pattern=[[-1, 128]], channel_multiplier=1).then_inc(setup_g, 1)
            pool.memset(minus_half[:, :], -0.5).then_inc(setup_g, 1)
            pool.memset(minus_one[:, :], -1.0).then_inc(setup_g, 1)
            pool.memset(eps[:, :], EPS).then_inc(setup_g, 1)
            pool.memset(kd_hi[:, :, :, :, :].rearrange("p k h g n -> p (k h g n)").bitcast(F32), 0.0).then_inc(setup_k, 1)
            pool.memset(kd_lo[:, :, :, :, :].rearrange("p k h g n -> p (k h g n)").bitcast(F32), 0.0).then_inc(setup_k, 1)

            def rstd(n, tiles, stats, ve, pow_, nm, done, normed):
                _, mv, v, rs, m, mr = tiles
                pool.wait_ge(stats, n + 1)
                if later(n):
                    pool.wait_ge(normed, n)
                pool.tensor_tensor(v[:, :], mv[:, :, 1], eps[:, :], ALU.add).then_inc(ve, 1)
                pool.tensor_tensor(m[:, :], mv[:, :, 0], minus_one[:, :], ALU.mult).then_inc(nm, 1)
                pool.wait_ge(ve, n + 1)
                pool.tensor_tensor(rs[:, :], v[:, :], minus_half[:, :], ALU.pow).then_inc(pow_, 1)
                pool.wait_ge(pow_, n + 1)
                pool.wait_ge(nm, n + 1)
                pool.tensor_tensor(mr[:, :], m[:, :], rs[:, :], ALU.mult).then_inc(done, 1)

            def c_rstd_part(g, k):
                rstd(2 * g + k, c_ln, c_stats, c_ve, c_pow, c_nm, c_rstd, c_done)

            def m_rstd_part(g, k):
                rstd(ATT_LNS * g + k, m_ln, m_stats, m_ve, m_pow, m_nm, m_rstd, m_done)

            def g_rstd_part(g):
                rstd(g, g_ln, g_stats, g_ve, g_pow, g_nm, g_rstd, g_done)

            def xb(g):
                if not later(g):
                    pool.wait_ge(ld_const, 16 * N_CONST)
                    pool.wait_ge(setup_g, 5)
                pool.wait_ge(x_loaded, 16 * (g + 1))
                if later(g):
                    pool.wait_ge(x2p, g)
                pool.tensor_tensor(x1[:, :, :], xin[:, :, :], b0_s[:, :].unsqueeze(1).to_broadcast((128, G, D)),
                                   ALU.add).then_inc(xb_done, 1)

            def e_norm_part(g):
                pool.wait_ge(e_rden, g + 1)
                pool.tensor_tensor(e_s, e_s, erd[:, :].unsqueeze(2).to_broadcast((128, G, N)), ALU.mult).then_inc(e_norm, 1)

            def x2b_part(g):
                pool.wait_ge(c_done, 2 * g + 2)
                if later(g):
                    pool.wait_ge(x3p, g)
                pool.tensor_tensor(x2b[:, :, :], x2[:, :, :], lbeta_s[:, :].unsqueeze(1).to_broadcast((128, G, D)),
                                   ALU.add).then_inc(x2b_done, 1)

            def p_norm(g, b):
                pool.wait_ge(sc_rden, G * g + b + 1)
                p = P[b % 2][:, :, :]
                pool.tensor_tensor(p, p, prd[b % 2][:, :].unsqueeze(2).to_broadcast((128, H, N)), ALU.mult).then_inc(sc_norm, 1)

            def residual(g):
                pool.wait_ge(o_biased, g + 1)
                pool.wait_ge(x2b_done, g + 1)
                pool.tensor_tensor(x2b[:, :, :], ob[:, :, :], x2b[:, :, :], ALU.add).then_inc(res_sum, 1)

            def times_gamma(g):
                pool.wait_ge(m_done, ATT_LNS * g + 1)
                pool.tensor_tensor(on[:, :, :], on[:, :, :], gamma_s[:, :].unsqueeze(1).to_broadcast((128, G, D)),
                                   ALU.mult).then_inc(on_scaled, 1)

            def rh_rest(g, s):
                pool.wait_ge(rh_hi, T * g + s + 1)
                pool.tensor_tensor(rlo[:, :, :, :], rt[:, :, :, :], rhi[:, :, :, :], ALU.subtract).then_inc(rh_lo, 1)

            run(POOL_ORDER, {"c_xb": xb, "c_rstd": c_rstd_part, "c_enorm": e_norm_part, "m_x2b": x2b_part, "m_pnorm": p_norm,
                             "m_rstd": m_rstd_part, "m_residual": residual, "m_gamma": times_gamma, "g_rlo": rh_rest,
                             "g_rstd": g_rstd_part}, pool.Fori)

        @block.scalar
        def _(act):
            def normalise(dst, src, tiles, rstd, n, done):
                rs, mr = tiles[3], tiles[5]
                act.wait_ge(rstd, n + 1)
                for b in range(G):
                    last = act.activation(dst[:, b, :], src[:, b, :], ACT.Identity, bias=mr[:, b:b + 1], scale=rs[:, b:b + 1])
                last.then_inc(done, 1)

            def y_hi_part(g):
                act.wait_ge(y_mm, g + 1)
                if later(g):
                    act.wait_ge(s2_mm, g)
                act.activation(chi[:, :, :, :], feat(CP), ACT.Copy).then_inc(y_hi, 1)

            def x1_norm(g):
                normalise(x1, x1, c_ln, c_rstd, 2 * g, c_done)

            def x1_hi_part(g):
                act.wait_ge(x1t_mm, g + 1)
                act.activation(chi[:, :, :, :], feat(CP), ACT.Copy).then_inc(x1_hi, 1)

            def h_copy(g, i):
                act.wait_ge(h_mm, 2 * g + i + 1)
                act.activation(s1[:, 2 * i:2 * i + 2], CP[:, :, D], ACT.Copy)
                act.activation(hs[:, 2 * i:2 * i + 2, :], CP[:, :, 0:D], ACT.Copy).then_inc(h_copied, 1)

            def e_exp_part(g):
                act.wait_ge(e_nm, g + 1)
                for b in range(G):
                    last = act.activation(e_s[:, b, :], e_s[:, b, :], ACT.Exp, bias=enm[:, b:b + 1],
                                          accum_out=eden[:, b:b + 1])
                last.then_inc(e_exp, 1)

            def et_copy(g):
                act.wait_ge(et_mm, g + 1)
                act.activation(et_s, CP[:, 1, :].rearrange("p (g n) -> p g n", g=G), ACT.Copy).then_inc(et_copied, 1)

            def elu_exp(g):
                act.wait_ge(el_min, g + 1)
                act.activation(mn[:, :, :], mn[:, :, :], ACT.Exp).then_inc(el_exp, 1)

            def x2_norm(g):
                if later(g):
                    act.wait_ge(x2t_mm, g)
                    act.wait_ge(x2b_done, g)
                normalise(x2, mn, c_ln, c_rstd, 2 * g + 1, c_done)

            def x2_hi_part(g):
                act.wait_ge(x2t_mm, g + 1)
                if later(g):
                    act.wait_ge(sc_mm, 4 * g)
                act.activation(fhi[:, :, :, :], feat(MP), ACT.Copy).then_inc(x2_hi, 1)

            def k_hi_part(g):
                act.wait_ge(k_mm, g + 1)
                if later(g):
                    act.wait_ge(proj_mm, g)
                act.activation(khi[:, :, :, :], feat(MP), ACT.Copy).then_inc(k_hi, 1)

            def v_copy(g):
                act.wait_ge(v_mm, g + 1)
                if later(g):
                    act.wait_ge(o_mm, 4 * g)
                act.activation(vs[:, :, :], node(MP), ACT.Copy).then_inc(v_copied, 1)

            def q_hi_part(g):
                act.wait_ge(q_mm, g + 1)
                act.activation(fhi[:, :, :, :], feat(MP), ACT.Copy).then_inc(q_hi, 1)

            def p_exp(g, b):
                act.wait_ge(sc_nm, G * g + b + 1)
                p = P[b % 2]
                for h_ in range(H):
                    last = act.activation(p[:, h_, :], p[:, h_, :], ACT.Exp, bias=pnm[b % 2][:, h_:h_ + 1],
                                          scale=SCALE, accum_out=pden[b % 2][:, h_:h_ + 1])
                last.then_inc(sc_exp, 1)

            def pt_copy(g, b):
                n = G * g + b
                act.wait_ge(pt_mm, n + 1)
                if b >= 2 or later(g):
                    act.wait_ge(o_mm, n - 1)
                act.activation(PT[b % 2][:, :, :], heads(MP), ACT.Copy).then_inc(pt_copied, 1)

            def o_hi_part(g, b):
                act.wait_ge(o_mm, G * g + b + 1)
                if b == 0:
                    act.wait_ge(k_spread, 256 * (g + 1))
                act.activation(khi[:, :, b, :], MP[:, 0, 0:KB * N].rearrange("p (k n) -> p k n", k=KB),
                               ACT.Copy).then_inc(o_hi, 1)

            def o_norm(g):
                if later(g):
                    act.wait_ge(m_done, ATT_LNS * g)
                normalise(on, ob, m_ln, m_rstd, ATT_LNS * g, m_done)

            def ht_part(g):
                act.wait_ge(x3t_mm, g + 1)
                if later(g):
                    act.wait_ge(h_new, 2 * T * g)
                    act.wait_ge(hn_mm, 2 * T * g)
                act.activation(ht[:, :, :, :], feat(MP), ACT.Copy).then_inc(ht_set, 1)

            def h0_hi_part(g):
                act.wait_ge(x3t_mm, g + 1)
                if later(g):
                    act.wait_ge(hu_mm, T * g)
                act.activation(hhi[:, :, :, :], feat(MP), ACT.Copy).then_inc(h0_hi, 1)

            def a_hi_part(g, s):
                act.wait_ge(a_mm, T * g + s + 1)
                act.activation(ahi[:, :, :, :], feat(GP), ACT.Copy).then_inc(a_hi, 1)

            def hu_copy(g, s):
                act.wait_ge(hu_mm, T * g + s + 1)
                act.activation(hu[:, :, :, :], feat(GQ), ACT.Copy).then_inc(hu_copied, 1)

            def r_tanh_part(g, s):
                act.wait_ge(r_sum, T * g + s + 1)
                for k_ in range(KB):
                    last = act.activation(rt[:, k_, :, :], rt[:, k_, :, :], ACT.Tanh, bias=bias_r[:, k_:k_ + 1], scale=0.5)
                last.then_inc(r_tanh, 1)

            def rh_hi_part(g, s):
                act.wait_ge(rh_done, T * g + s + 1)
                act.activation(rhi[:, :, :, :], rt[:, :, :, :], ACT.Copy).then_inc(rh_hi, 1)

            def z_tanh_part(g, s):
                act.wait_ge(z_sum, T * g + s + 1)
                for k_ in range(KB):
                    last = act.activation(zt[:, k_, :, :], zt[:, k_, :, :], ACT.Tanh, bias=bias_z[:, k_:k_ + 1], scale=0.5)
                last.then_inc(z_tanh, 1)

            def hv_tanh_part(g, s, k_):
                act.wait_ge(hv_mm, KB * (T * g + s) + k_ + 1)
                if s == 0 and later(g):
                    act.wait_ge(stored, 16 * g)
                act.activation(hv[:, k_, :, :], feat(GP)[:, k_, :, :], ACT.Tanh, bias=bias_v[:, k_:k_ + 1]).then_inc(hv_tanh, 1)

            def h_hi_part(g, s, k_):
                act.wait_ge(h_new, KB * (T * g + s) + k_ + 1)
                act.activation(hhi[:, k_, :, :], ht[:, k_, :, :], ACT.Copy).then_inc(h_hi, 1)

            def hn_copy(g, s):
                act.wait_ge(hn_mm, KB * (T * g + s) + KB)
                act.activation(hn[:, :, :], node(GQ), ACT.Copy).then_inc(hn_copied, 1)

            def res_norm(g):
                normalise(res, res, g_ln, g_rstd, g, g_done)

            act.wait_ge(setup_v, 3)
            run(SCALAR_ORDER, {"c_yhi": y_hi_part, "c_norm0": x1_norm, "c_x1hi": x1_hi_part, "c_hcopy": h_copy,
                               "c_exp": e_exp_part, "c_etcopy": et_copy, "c_eluexp": elu_exp, "c_norm1": x2_norm,
                               "m_x2hi": x2_hi_part, "m_khi": k_hi_part, "m_vcopy": v_copy, "m_qhi": q_hi_part,
                               "m_exp": p_exp, "m_ptcopy": pt_copy, "m_ohi": o_hi_part, "m_norm0": o_norm,
                               "m_ht": ht_part, "m_h0hi": h0_hi_part, "g_ahi": a_hi_part, "g_hucopy": hu_copy,
                               "g_rtanh": r_tanh_part, "g_rhi": rh_hi_part, "g_ztanh": z_tanh_part,
                               "g_vtanh": lambda g, n: hv_tanh_part(g, n // KB, n % KB),
                               "g_hhi": lambda g, n: h_hi_part(g, n // KB, n % KB),
                               "g_hncopy": hn_copy, "g_norm": res_norm}, act.Fori)

        @block.vector
        def _(dve):
            dve.wait_ge(ld_const, 16 * N_CONST)
            dve.wait_ge(ld_w, 16 * N_W)
            for dst, n1, n2, f in ((bias_z, 0, 1, 0.5), (bias_r, 2, 1, 0.5), (bias_v, 3, 4, 1.0)):
                dve.tensor_tensor(dst[:, :], gb[:, n1, :], gb[:, n2, :], ALU.add).then_inc(setup_d, 1)
            dve.wait_ge(setup_d, 3)
            for dst, f in ((bias_z, 0.5), (bias_r, 0.5), (bias_v, 1.0)):
                dve.tensor_scalar(dst[:, :], dst[:, :], f, None, ALU.mult).then_inc(setup_v, 1)
            dve.tensor_scalar(mask[:, :], adj_s[:, :], 0.0, MASKED, ALU.is_equal, ALU.mult).then_inc(setup_d, 1)
            for w in (raw_3, raw_4, raw_5):
                dve.tensor_tensor(w[0], w[0], w[1], ALU.add).then_inc(setup_d, 1)
            dve.tensor_scalar(raw_u5, raw_u5, 0.5, None, ALU.mult).then_inc(setup_d, 1)
            for k_ in range(KB):
                for t_ in range(2):
                    dve.wait_ge(setup_d, 8 + 2 * k_ + t_)
                    dve.tensor_tensor_reduce(raw(vs, 1)[:, 0, :], raw_w1[:, k_, :], a_row[:, t_, :], 1.0, 0.0, ALU.mult, ALU.add,
                                             wa[:, k_, t_:t_ + 1]).then_inc(setup_d, 1)
            dve.wait_ge(setup_d, 12)
            for w, src in ((W0, raw_w0), (WQ, raw_q), (WK, raw_k), (WV, raw_v), (WP, raw_p), (W3, raw_3[0]),
                           (W4, raw_4[0]), (W5, raw_5[0]), (U3, raw_u3), (U5, raw_u5)):
                dve.tensor_copy(w[0][:, :, :], src).then_inc(setup_d, 1)
            dve.tensor_copy(W1[0][:, :, 0:D], raw_w1).then_inc(setup_d, 1)
            dve.tensor_copy(W1[0][:, :, D:D + 2], wa[:, :, :]).then_inc(setup_d, 1)
            wa2 = wa[:, :, 1:2].to_broadcast((128, KB, 128))
            dve.tensor_copy(WA2[0][:, :, :], wa2).then_inc(setup_d, 1)
            dve.wait_ge(setup_d, 25)
            for w, src in ((W0, raw_w0), (WQ, raw_q), (WK, raw_k), (WV, raw_v), (WP, raw_p), (W3, raw_3[0]),
                           (W4, raw_4[0]), (W5, raw_5[0]), (U3, raw_u3), (U5, raw_u5)):
                dve.tensor_tensor(w[1][:, :, :], src, w[0][:, :, :], ALU.subtract).then_inc(setup_v, 1)
            dve.tensor_tensor(W1[1][:, :, 0:D], raw_w1, W1[0][:, :, 0:D], ALU.subtract).then_inc(setup_v, 1)
            dve.tensor_tensor(W1[1][:, :, D:D + 2], wa[:, :, :], W1[0][:, :, D:D + 2], ALU.subtract).then_inc(setup_v, 1)
            dve.tensor_tensor(WA2[1][:, :, :], wa2, WA2[0][:, :, :], ALU.subtract).then_inc(setup_v, 1)
            dve.wait_ge(setup_v, 16)

            def wait_apart(signal, value, spot):
                dve.wait_ge(signal, value)
                dve.memset(unused[:, spot:spot + 1], 0.0)

            def stats(src, tiles, bn, n, done, used, spot):
                st, mv = tiles[0], tiles[1]
                if later(n):
                    dve.wait_ge(used, n)
                for b in range(G):
                    dve.bn_stats(st[:, b, :], src[:, b, :]).then_inc(bn, 1)
                wait_apart(bn, G * n + G, spot)
                for b in range(G):
                    last = dve.bn_aggr(mv[:, b, :], st[:, b, :])
                last.then_inc(done, 1)

            def y_lo_part(g):
                dve.wait_ge(y_hi, g + 1)
                dve.tensor_tensor(clo[:, :, :, :], feat(CP), chi[:, :, :, :], ALU.subtract).then_inc(y_lo, 1)

            def x1_stats(g):
                dve.wait_ge(out0_mm, g + 1)
                dve.wait_ge(xb_done, g + 1)
                dve.tensor_tensor(x1[:, :, :], node(CP), x1[:, :, :], ALU.add).then_inc(x1p, 1)
                dve.wait_ge(x1p, g + 1)
                stats(x1, c_ln, c_bn, 2 * g, c_stats, c_rstd, 0)

            def x1_lo_part(g):
                dve.wait_ge(x1_hi, g + 1)
                dve.tensor_tensor(clo[:, :, :, :], feat(CP), chi[:, :, :, :], ALU.subtract).then_inc(x1_lo, 1)

            def scores1(g):
                dve.wait_ge(s2_mm, g + 1)
                if later(g):
                    dve.wait_ge(c_done, 2 * g)
                ps = CP[:, 0, :].rearrange("p (g n) -> p g n", g=G)
                dve.tensor_tensor(e_s, ps, s1[:, :].unsqueeze(2).to_broadcast((128, G, N)), ALU.add).then_inc(e_sum, 1)
                dve.wait_ge(e_sum, g + 1)
                dve.scalar_tensor_tensor(out=e_s, in0=e_s, scalar=SLOPE, in1=e_s, op0=ALU.mult, op1=ALU.max).then_inc(e_leaky, 1)
                wait_apart(e_leaky, g + 1, 1)
                for b in range(G):
                    last = dve.tensor_tensor_reduce(e_s[:, b, :], e_s[:, b, :], adj_s[:, :], 1.0, LOWEST, ALU.mult,
                                                    ALU.max, emax[:, b:b + 1])
                last.then_inc(e_max, 1)
                dve.wait_ge(e_max, g + 1)
                dve.tensor_scalar(enm[:, :], emax[:, :], -1.0, None, ALU.mult).then_inc(e_nm, 1)

            def e_reciprocal(g):
                dve.wait_ge(e_exp, g + 1)
                dve.reciprocal(erd[:, :], eden[:, :]).then_inc(e_rden, 1)

            def elu_in(g):
                dve.wait_ge(hp_mm, g + 1)
                dve.scalar_tensor_tensor(out=el[:, :, :], in0=hs[:, :, :], scalar=beta_s[:, 0:1], in1=node(CP),
                                         op0=ALU.mult, op1=ALU.add).then_inc(el_sum, 1)
                dve.wait_ge(el_sum, g + 1)
                dve.tensor_scalar(mn[:, :, :], el[:, :, :], 0.0, None, ALU.min).then_inc(el_min, 1)

            def elu_out(g):
                dve.wait_ge(el_exp, g + 1)
                dve.scalar_tensor_tensor(out=el[:, :, :], in0=el[:, :, :], scalar=0.0, in1=mn[:, :, :],
                                         op0=ALU.max, op1=ALU.add).then_inc(el_pos, 1)
                dve.wait_ge(el_pos, g + 1)
                dve.scalar_tensor_tensor(out=mn[:, :, :], in0=el[:, :, :], scalar=-1.0, in1=x1[:, :, :],
                                         op0=ALU.add, op1=ALU.add).then_inc(x2p, 1)

            def x2_stats(g):
                dve.wait_ge(x2p, g + 1)
                stats(mn, c_ln, c_bn, 2 * g + 1, c_stats, c_rstd, 0)

            def x2_lo_part(g):
                dve.wait_ge(x2_hi, g + 1)
                dve.tensor_tensor(flo[:, :, :, :], feat(MP), fhi[:, :, :, :], ALU.subtract).then_inc(x2_lo, 1)

            def k_lo_part(g):
                dve.wait_ge(k_hi, g + 1)
                dve.tensor_tensor(klo[:, :, :, :], feat(MP), khi[:, :, :, :], ALU.subtract).then_inc(k_lo, 1)

            def q_lo_part(g):
                dve.wait_ge(q_hi, g + 1)
                dve.tensor_tensor(flo[:, :, :, :], feat(MP), fhi[:, :, :, :], ALU.subtract).then_inc(q_lo, 1)

            def p_max(g, b):
                n = G * g + b
                if b >= 2 or later(g):
                    dve.wait_ge(pt_mm, n - 1)
                wait_apart(sc_mm, n + 1, 2)
                p = P[b % 2]
                for h_ in range(H):
                    last = dve.tensor_tensor_reduce(p[:, h_, :], heads(MP)[:, h_, :], mask[:, :], 1.0, LOWEST, ALU.add,
                                                    ALU.max, pmax[b % 2][:, h_:h_ + 1])
                last.then_inc(sc_max, 1)
                dve.wait_ge(sc_max, n + 1)
                dve.tensor_scalar(pnm[b % 2][:, :], pmax[b % 2][:, :], -SCALE, None, ALU.mult).then_inc(sc_nm, 1)

            def p_reciprocal(g, b):
                dve.wait_ge(sc_exp, G * g + b + 1)
                dve.reciprocal(prd[b % 2][:, :], pden[b % 2][:, :]).then_inc(sc_rden, 1)

            def o_lo_part(g, b):
                dve.wait_ge(o_hi, G * g + b + 1)
                ps = MP[:, 0, 0:KB * N].rearrange("p (k n) -> p k n", k=KB)
                dve.tensor_tensor(klo[:, :, b, :], ps, khi[:, :, b, :], ALU.subtract).then_inc(o_lo, 1)

            def o_stats(g):
                dve.wait_ge(proj_mm, g + 1)
                if later(g):
                    dve.wait_ge(res_sum, g)
                dve.tensor_tensor(ob[:, :, :], node(MP), bp_s[:, :].unsqueeze(1).to_broadcast((128, G, D)),
                                  ALU.add).then_inc(o_biased, 1)
                dve.wait_ge(o_biased, g + 1)
                stats(ob, m_ln, m_bn, ATT_LNS * g, m_stats, m_rstd, 3)

            def x3_sum(g):
                dve.wait_ge(on_scaled, g + 1)
                dve.wait_ge(res_sum, g + 1)
                dve.tensor_tensor(on[:, :, :], x2b[:, :, :], on[:, :, :], ALU.add).then_inc(x3p, 1)

            def x3_stats(g):
                dve.wait_ge(x3p, g + 1)
                stats(on, m_ln, m_bn, ATT_LNS * g + 1, m_stats, m_rstd, 3)

            def x3_norm(g):
                dve.wait_ge(m_rstd, ATT_LNS * g + 2)
                if later(g):
                    dve.wait_ge(res_done, g)
                for b in range(G):
                    last = dve.tensor_scalar(x3[:, b, :], on[:, b, :], m_ln[3][:, b:b + 1], m_ln[5][:, b:b + 1],
                                             ALU.mult, ALU.add)
                last.then_inc(m_done, 1)

            def h0_lo_part(g):
                dve.wait_ge(h0_hi, g + 1)
                dve.wait_ge(ht_set, g + 1)
                dve.tensor_tensor(hlo[:, :, :, :], ht[:, :, :, :], hhi[:, :, :, :], ALU.subtract).then_inc(h0_lo, 1)

            def a_lo_part(g, s):
                dve.wait_ge(a_hi, T * g + s + 1)
                dve.tensor_tensor(alo[:, :, :, :], feat(GP), ahi[:, :, :, :], ALU.subtract).then_inc(a_lo, 1)

            def r_sum_part(g, s):
                n = T * g + s
                dve.wait_ge(r_mm, n + 1)
                dve.wait_ge(hu_copied, n + 1)
                dve.tensor_tensor(rt[:, :, :, :], feat(GP), hu[:, :, :, :], ALU.add).then_inc(r_sum, 1)

            def rh_part(g, s):
                dve.wait_ge(r_tanh, T * g + s + 1)
                dve.scalar_tensor_tensor(out=rt[:, :, :, :], in0=rt[:, :, :, :], scalar=1.0, in1=ht[:, :, :, :],
                                         op0=ALU.add, op1=ALU.mult).then_inc(rh_done, 1)

            def z_sum_part(g, s):
                dve.wait_ge(z_mm, T * g + s + 1)
                dve.tensor_tensor(zt[:, :, :, :], feat(GQ), hu[:, :, :, :], ALU.add).then_inc(z_sum, 1)

            def h_update(g, s, k_):
                n = KB * (T * g + s) + k_
                v_, h_ = hv[:, k_, :, :], ht[:, k_, :, :]
                dve.wait_ge(hv_tanh, n + 1)
                dve.tensor_tensor(v_, v_, h_, ALU.subtract).then_inc(hv_diff, 1)
                dve.wait_ge(z_tanh, T * g + s + 1)
                dve.wait_ge(hv_diff, n + 1)
                dve.scalar_tensor_tensor(out=v_, in0=zt[:, k_, :, :], scalar=1.0, in1=v_,
                                         op0=ALU.add, op1=ALU.mult).then_inc(hv_scaled, 1)
                dve.wait_ge(hv_scaled, n + 1)
                dve.scalar_tensor_tensor(out=h_, in0=v_, scalar=0.5, in1=h_,
                                         op0=ALU.mult, op1=ALU.add).then_inc(h_new, 1)

            def h_lo_part(g, s, k_):
                dve.wait_ge(h_hi, KB * ((T - 1) * g + s) + k_ + 1)
                dve.tensor_tensor(hlo[:, k_, :, :], ht[:, k_, :, :], hhi[:, k_, :, :], ALU.subtract).then_inc(h_lo, 1)

            def res_sum_part(g):
                dve.wait_ge(hn_mm, KB * (T * g + T))
                dve.tensor_tensor(res, node(GQ), x3[:, :, :], ALU.add).then_inc(res_done, 1)

            def res_stats(g):
                dve.wait_ge(res_done, g + 1)
                stats(res, g_ln, g_bn, g, g_stats, g_rstd, 4)

            run(VECTOR_ORDER, {"c_ylo": y_lo_part, "c_stats0": x1_stats, "c_x1lo": x1_lo_part, "c_scores": scores1,
                               "c_erd": e_reciprocal, "c_eluin": elu_in, "c_eluout": elu_out, "c_stats1": x2_stats,
                               "m_x2lo": x2_lo_part, "m_klo": k_lo_part, "m_qlo": q_lo_part, "m_max": p_max,
                               "m_prd": p_reciprocal, "m_olo": o_lo_part, "m_stats0": o_stats, "m_x3sum": x3_sum,
                               "m_stats1": x3_stats, "m_norm1": x3_norm, "m_h0lo": h0_lo_part, "g_alo": a_lo_part,
                               "g_rsum": r_sum_part, "g_rh": rh_part, "g_zsum": z_sum_part,
                               "g_update": lambda g, n: h_update(g, n // KB, n % KB),
                               "g_hlo": lambda g, n: h_lo_part(g, n // KB, n % KB),
                               "g_res": res_sum_part, "g_stats": res_stats}, dve.Fori)

        @block.tensor
        def _(pe):
            def features(ps, w, hi, lo):
                for o in range(KB):
                    for k_ in range(KB):
                        cols = slice(o * 128, o * 128 + 128)
                        last = three(pe, ps[:, o, :], (w[0][:, k_, cols], w[1][:, k_, cols]),
                                     (flat(hi, k_), flat(lo, k_)), k_ == 0, k_ == KB - 1)
                return last

            def flat(tile, k_):
                return tile[:, k_, :, :].rearrange("p g n -> p (g n)")

            def nodes(dst, graphs, w, hi, lo, width=D):
                for b in graphs:
                    for k_ in range(KB):
                        last = three(pe, dst(b), (hi[:, k_, b, :], lo[:, k_, b, :]),
                                     (w[0][:, k_, 0:width], w[1][:, k_, 0:width]), k_ == 0, k_ == KB - 1)
                return last

            def turn_nodes(ps, src):
                for k_ in range(KB):
                    for b in range(G):
                        last = pe.transpose(feat(ps)[:, k_, b, :], src[:, b, k_ * 128:k_ * 128 + 128], ident[:, :])
                return last

            def times_adj(ps, src):
                for k_ in range(KB):
                    for b in range(G):
                        last = pe.matmul(feat(ps)[:, k_, b, :], src[:, b, k_ * 128:k_ * 128 + 128], adjt_s[:, :],
                                         start=True, stop=True)
                return last

            def y(g):
                pe.wait_ge(x_loaded, 16 * (g + 1))
                if later(g):
                    pe.wait_ge(el_sum, g)
                times_adj(CP, xin).then_inc(y_mm, 1)

            def out0(g):
                pe.wait_ge(y_lo, g + 1)
                nodes(lambda b: node(CP)[:, b, :], range(G), W0, chi, clo).then_inc(out0_mm, 1)

            def x1t(g):
                pe.wait_ge(c_done, 2 * g + 1)
                turn_nodes(CP, x1).then_inc(x1t_mm, 1)

            def h(g, i):
                if i == 0:
                    pe.wait_ge(x1_lo, g + 1)
                else:
                    pe.wait_ge(h_copied, 2 * g + 1)
                nodes(lambda b: CP[:, b % 2, 0:D + 2], range(2 * i, 2 * i + 2), W1, chi, clo, D + 2).then_inc(h_mm, 1)

            def s2(g):
                pe.wait_ge(h_copied, 2 * g + 2)
                for k_ in range(KB):
                    last = three(pe, CP[:, 0, :], (WA2[0][:, k_, :], WA2[1][:, k_, :]),
                                 (flat(chi, k_), flat(clo, k_)), k_ == 0, k_ == KB - 1)
                last.then_inc(s2_mm, 1)

            def et(g):
                pe.wait_ge(e_norm, g + 1)
                for b in range(G):
                    last = pe.transpose(CP[:, 1, b * N:b * N + N], e_s[:, b, :], ident[:, :])
                last.then_inc(et_mm, 1)

            def hp(g):
                pe.wait_ge(et_copied, g + 1)
                for b in range(G):
                    last = pe.matmul(node(CP)[:, b, :], et_s[:, b, :], hs[:, b, :], start=True, stop=True)
                last.then_inc(hp_mm, 1)

            def x2t(g):
                pe.wait_ge(c_done, 2 * g + 2)
                if later(g):
                    pe.wait_ge(ht_set, g)
                    pe.wait_ge(h0_hi, g)
                turn_nodes(MP, x2).then_inc(x2t_mm, 1)

            def k(g):
                pe.wait_ge(x2_lo, g + 1)
                features(MP, WK, fhi, flo).then_inc(k_mm, 1)

            def v(g):
                pe.wait_ge(k_lo, g + 1)
                nodes(lambda b: node(MP)[:, b, :], range(G), WV, fhi, flo).then_inc(v_mm, 1)

            def q(g):
                pe.wait_ge(v_copied, g + 1)
                features(MP, WQ, fhi, flo).then_inc(q_mm, 1)

            def score(g, b):
                n = G * g + b
                if b == 0:
                    pe.wait_ge(q_lo, g + 1)
                if b == 1:
                    pe.wait_ge(sc_max, n)
                if b % 2 == 0:
                    pe.wait_ge(k_spread, 256 * g + 128 * (b // 2 + 1))
                if b >= 2:
                    pe.wait_ge(o_lo, n - 1)
                for k_ in range(KB):
                    last = three(pe, MP[:, k_, :], (fhi[:, k_, b, :], flo[:, k_, b, :]),
                                 (kd_hi[:, k_, :, b % 2, :], kd_lo[:, k_, :, b % 2, :]), True, True)
                last.then_inc(sc_mm, 1)

            def turn(g, b):
                n = G * g + b
                pe.wait_ge(sc_norm, n + 1)
                if b < G - 1:
                    pe.wait_ge(sc_max, n + 2)
                else:
                    pe.wait_ge(o_lo, n)
                for h_ in range(H):
                    last = pe.transpose(heads(MP)[:, h_, :], P[b % 2][:, h_, :], ident[:, :])
                last.then_inc(pt_mm, 1)

            def mix(g, b):
                n = G * g + b
                pe.wait_ge(pt_copied, n + 1)
                for k_ in range(KB):
                    for h_ in range(HB):
                        f = k_ * 128 + h_ * HD
                        last = pe.matmul(MP[h_ * HD:h_ * HD + HD, 0, k_ * N:k_ * N + N],
                                         vs[:, b, f:f + HD], PT[b % 2][:, k_ * HB + h_, :], start=True, stop=True)
                last.then_inc(o_mm, 1)

            def proj(g):
                pe.wait_ge(o_lo, G * g + G)
                nodes(lambda b: node(MP)[:, b, :], range(G), WP, khi, klo).then_inc(proj_mm, 1)

            def x3t(g):
                pe.wait_ge(m_done, ATT_LNS * g + 2)
                turn_nodes(MP, x3).then_inc(x3t_mm, 1)

            def a(g, s):
                n = T * g + s
                if s:
                    pe.wait_ge(hn_copied, (T - 1) * g + s)
                    pe.wait_ge(hv_tanh, KB * n)
                else:
                    pe.wait_ge(m_done, ATT_LNS * g + 2)
                    if later(g):
                        pe.wait_ge(hv_tanh, KB * n)
                times_adj(GP, hn if s else x3).then_inc(a_mm, 1)

            def hu_part(g, s):
                if s:
                    pe.wait_ge(h_lo, KB * ((T - 1) * g + s))
                    pe.wait_ge(hn_copied, (T - 1) * g + s)
                else:
                    pe.wait_ge(h0_lo, g + 1)
                    if later(g):
                        pe.wait_ge(res_done, g)
                features(GQ, U3, hhi, hlo).then_inc(hu_mm, 1)

            def r(g, s):
                pe.wait_ge(a_lo, T * g + s + 1)
                features(GP, W4, ahi, alo).then_inc(r_mm, 1)

            def z(g, s):
                pe.wait_ge(hu_copied, T * g + s + 1)
                pe.wait_ge(a_lo, T * g + s + 1)
                features(GQ, W3, ahi, alo).then_inc(z_mm, 1)

            def one_block(o, w, hi, lo, start, stop):
                for k_ in range(KB):
                    cols = slice(o * 128, o * 128 + 128)
                    last = three(pe, GP[:, o, :], (w[0][:, k_, cols], w[1][:, k_, cols]),
                                 (flat(hi, k_), flat(lo, k_)), start and k_ == 0, stop and k_ == KB - 1)
                return last

            def v5(g, s):
                pe.wait_ge(r_sum, T * g + s + 1)
                for o in range(KB):
                    one_block(o, W5, ahi, alo, True, False)

            def u5(g, n):
                s, o = n // KB, n % KB
                if o == 0:
                    pe.wait_ge(rh_lo, T * g + s + 1)
                one_block(o, U5, rhi, rlo, False, True).then_inc(hv_mm, 1)

            def hn_turn(g, n):
                s, k_ = n // KB, n % KB
                pe.wait_ge(h_new, KB * (T * g + s) + k_ + 1)
                if k_ == 0:
                    pe.wait_ge(z_sum, T * g + s + 1)
                for b in range(G):
                    last = pe.transpose(node(GQ)[:, b, k_ * 128:k_ * 128 + 128], ht[:, k_, b, :], ident[:, :])
                last.then_inc(hn_mm, 1)

            pe.wait_ge(ld_const, 16 * N_CONST)
            pe.wait_ge(setup_v, 16)
            pe.wait_ge(setup_g, 2)
            run(TENSOR_ORDER, {"c_y": y, "c_out0": out0, "c_x1t": x1t, "c_h": h, "c_s2": s2, "c_et": et, "c_hp": hp,
                               "m_x2t": x2t, "m_k": k, "m_v": v, "m_q": q, "m_score": score, "m_turn": turn,
                               "m_mix": mix, "m_proj": proj, "m_x3t": x3t, "g_a": a, "g_hu": hu_part, "g_r": r,
                               "g_z": z, "g_v": v5, "g_u5": u5, "g_turn": hn_turn}, pe.Fori)


def kernel(**inputs):
    import numpy as _np
    import concourse.bacc as _bacc
    from concourse import mybir as _mybir
    from concourse.bass_utils import run_bass_kernel_spmd as _run

    i = {k: _np.asarray(v) for k, v in inputs.items()}

    def by_block(v):
        return v.reshape(KB, 128).T

    arrays = {
        "x": i["x"], "adj": i["adj"], "adj_t": i["adj"].T,
        "w0": i["L0_gnn_weight"], "b0": i["L0_gnn_bias"],
        "w1": i["L1_gnn_W"], "a_vec": i["L1_gnn_a"].reshape(2, D), "beta": i["L1_gnn_beta"],
        "wqkv": i["L2_gnn_w_qkv"], "wp": i["L2_gnn_w_proj"], "bp": i["L2_gnn_b_proj"],
        "gamma": i["L2_gnn_ln_gamma"], "lbeta": i["L2_gnn_ln_beta"],
        "w3": i["L3_gnn_w3_w"].T, "w4": i["L3_gnn_w4_w"].T, "w5": i["L3_gnn_w5_w"].T,
        "u3": i["L3_gnn_u3_w"].T, "u5": i["L3_gnn_u5_w"].T,
        "gate_bias": _np.stack([by_block(i[f"L3_gnn_{n}_b"]) for n in ("w3", "u3", "w4", "w5", "u5")]),
    }
    nc = _bacc.Bacc("TRN2", target_bir_lowering=False, num_devices=1)
    ins, args = {}, []
    for name, a in arrays.items():
        a = _np.ascontiguousarray(a)
        ins[f"in_{name}"] = a
        args.append(nc.dram_tensor(f"in_{name}", a.shape, _mybir.dt.from_np(a.dtype), kind="ExternalInput").ap())
    args.append(nc.dram_tensor("out", (B, N, D), _mybir.dt.float32, kind="ExternalOutput").ap())
    gnn_stack(nc, *args)
    r = _run(nc, [ins], core_ids=[0])
    return r.results[0]["out"]
```

```python
import concourse.bass as bass
from concourse import mybir
from contextlib import ExitStack

B, N, D = 64, 128, 256
G = 4
NG = B // G
KB = D // 128
H = 8
HD = D // H
HB = 128 // HD
T = 3
SCALE = float(HD) ** -0.5
SLOPE = 0.2
EPS = 1e-5
MASKED = -1e30
LOWEST = -3e38

TENSOR_ORDER = """
    c_y.0+3 m_x3t+1 g_a.0+1 g_a.1+1 m_x2t.0+2 m_x2t.1+2 c_y.1+3 g_turn.4+0 g_turn.5+0 m_k.0+2 m_k.1+2
    g_hu.0+1 m_v.0+2 m_v.1+2 m_q.0+2 m_q.1+2 c_out0.0+3 g_hu.1+1 g_r.0+1 m_score.0+2 c_out0.1+3
    m_score.1+2 g_r.1+1 g_z.0+1 m_score.2+2 g_v.0+1 g_z.1+1 m_score.3+2 c_x1t.0+3 c_x1t.1+3 g_v.1+1
    g_u5.0+1 g_u5.1+1 m_turn.0+2 m_turn.1+2 c_h.0+3 c_h.1+3 g_turn.0+1 m_mix.0+2 c_h.2+3 g_a.2+1
    g_turn.1+1 m_score.4+2 c_h.3+3 m_score.5+2 g_hu.2+1 g_a.3+1 m_turn.2+2 c_s2+3 g_hu.3+1 m_turn.3+2
    g_r.2+1 g_r.3+1 m_mix.1+2 g_z.2+1 m_score.6+2 c_et+3 m_score.7+2 g_v.2+1 c_hp.0+3 g_v.3+1 g_u5.2+1
    m_turn.4+2 m_turn.5+2 g_z.3+1 m_mix.2+2 g_u5.3+1 g_turn.2+1 m_turn.6+2 m_turn.7+2 c_hp.1+3 m_mix.3+2
    g_a.4+1 m_proj.0+2 g_turn.3+1 m_proj.1+2 g_a.5+1 g_hu.4+1 g_hu.5+1 g_r.4+1 g_r.5+1 g_v.4+1 g_z.4+1
    g_z.5+1 g_v.5+1 g_u5.4+1 g_u5.5+1
"""
SCALAR_ORDER = """
    c_yhi.0+3 c_yhi.1+3 m_vcopy.1+2 m_qhi.0+2 m_qhi.1+2 g_hucopy.1+1 g_norm+0 m_exp.0+2 g_rtanh.0+1
    c_norm0.0+3 m_exp.1+2 g_rtanh.1+1 c_norm0.1+3 g_rhi.0+1 g_rhi.1+1 g_ztanh.0+1 c_x1hi.0+3 c_x1hi.1+3
    m_exp.2+2 g_vtanh.0+1 g_ztanh.1+1 g_vtanh.1+1 m_ptcopy.0+2 m_ptcopy.1+2 c_hcopy.0+3 g_hhi.0+1
    c_hcopy.1+3 g_hncopy.0+1 m_ohi.0+2 g_hhi.1+1 m_exp.3+2 g_hncopy.1+1 g_ahi.2+1 c_hcopy.2+3 c_hcopy.3+3
    m_exp.4+2 g_ahi.3+1 g_hucopy.2+1 m_ptcopy.2+2 m_exp.5+2 m_ptcopy.3+2 g_hucopy.3+1 c_exp+3 g_rtanh.2+1
    m_ohi.1+2 g_rtanh.3+1 g_rhi.2+1 g_rhi.3+1 c_etcopy+3 m_exp.6+2 m_exp.7+2 c_eluexp.0+3 g_ztanh.2+1
    g_vtanh.2+1 m_ptcopy.4+2 m_ptcopy.5+2 m_ohi.2+2 g_hhi.2+1 g_ztanh.3+1 g_vtanh.3+1 m_ptcopy.6+2
    m_ptcopy.7+2 g_hncopy.2+1 m_ohi.3+2 g_ahi.4+1 g_hhi.3+1 g_hncopy.3+1 c_eluexp.1+3 c_norm1.0+3
    g_ahi.5+1 m_norm0.0+2 g_hucopy.4+1 g_hucopy.5+1 g_rtanh.4+1 m_norm0.1+2 g_rtanh.5+1 g_rhi.4+1
    c_norm1.1+3 g_rhi.5+1 g_ztanh.4+1 g_vtanh.4+1 g_vtanh.5+1 g_ztanh.5+1 m_ht+2 m_h0hi+2 m_x2hi.0+3
    m_x2hi.1+3 g_ahi.0+2 m_khi.0+3 m_khi.1+3 g_ahi.1+2 g_hucopy.0+2 m_vcopy.0+3
"""
VECTOR_ORDER = """
    c_ylo.0+3 c_ylo.1+3 g_stats+0 m_qlo.0+2 m_qlo.1+2 c_x1sum.0+3 c_stats.0+3 m_max.0+2 g_rsum.0+1
    c_x1sum.1+3 c_stats.1+3 m_max.1+2 g_rsum.1+1 g_zsum.0+1 g_rh.0+1 m_max.2+2 g_rh.1+1 m_prd.0+2
    m_prd.1+2 g_rlo.0+1 g_rlo.1+1 m_max.3+2 c_x1lo.0+3 g_zsum.1+1 c_x1lo.1+3 g_update.0+1 g_update.1+1
    m_olo.0+2 g_hlo.0+1 m_prd.2+2 g_hlo.1+1 m_max.4+2 m_max.5+2 g_alo.2+1 m_prd.3+2 g_alo.3+1 c_scores+3
    g_rsum.2+1 g_rsum.3+1 m_prd.4+2 m_prd.5+2 c_erd+3 m_olo.1+2 g_rh.2+1 g_rh.3+1 m_max.6+2 g_rlo.2+1
    m_max.7+2 g_rlo.3+1 c_eluin.0+3 m_prd.6+2 g_zsum.2+1 m_prd.7+2 c_eluout.0+3 g_update.2+1 g_zsum.3+1
    m_olo.2+2 g_hlo.2+1 c_stats.2+3 g_update.3+1 m_olo.3+2 c_eluin.1+3 g_alo.4+1 m_obias.0+2 g_hlo.3+1
    m_stats.0+2 m_obias.1+2 c_eluout.1+3 g_alo.5+1 m_stats.1+2 c_stats.3+3 g_rsum.4+1 m_x3sum.0+2
    g_rsum.5+1 g_rh.4+1 m_stats.2+2 g_rh.5+1 g_rlo.4+1 m_x3sum.1+2 g_rlo.5+1 m_stats.3+2 g_zsum.4+1
    g_zsum.5+1 m_norm1.0+2 m_norm1.1+2 g_update.4+1 g_update.5+1 m_x2lo.0+3 m_x2lo.1+3 m_h0lo+2 g_res+1
    m_klo.0+3 m_klo.1+3 g_alo.0+2 g_alo.1+2
"""
POOL_ORDER = """
    c_xb+3 g_rstd+0 m_x2b+2 m_keep+1 c_rstd.0+3 c_rstd.1+3 m_pnorm.0+2 m_pnorm.1+2 m_pnorm.2+2 m_pnorm.3+2
    c_enorm+3 m_pnorm.4+2 m_pnorm.5+2 m_pnorm.6+2 m_pnorm.7+2 c_rstd.2+3 m_residual.0+2 m_rstd.0+2
    m_residual.1+2 m_gamma.0+2 m_rstd.1+2 c_rstd.3+3 m_gamma.1+2 m_rstd.2+2 m_rstd.3+2
"""
SYNC_ORDER = "c_load+4 m_spread.0+2 g_store+0 m_spread.1+2"
AHEAD = 4


def gnn_stack(nc, x, adj, adj_t, w0, b0, w1, a_vec, beta, wqkv, wp, bp, gamma, lbeta,
              w3, w4, w5, u3, u5, gate_bias, out):
    F32, F32R = mybir.dt.float32, mybir.dt.float32r
    ALU, ACT = mybir.AluOpType, mybir.ActivationFunctionType

    ctx = ExitStack()
    with ctx:
        def sb(name, shape, dt=F32):
            return ctx.enter_context(nc.sbuf_tensor(name, shape, dt))

        def sem(name):
            return ctx.enter_context(nc.semaphore(name))

        def pair(name, shape):
            return sb(name + "_hi", shape, F32R), sb(name + "_lo", shape, F32R)

        W0, WQ, WK, WV, WP = (pair(n, [128, KB, D]) for n in ("w0", "wq", "wk", "wv", "wp"))
        W3, W4, W5, U3, U5 = (pair(n, [128, KB, D]) for n in ("w3", "w4", "w5", "u3", "u5"))
        W1 = pair("w1", [128, KB, D + 2])
        adj_s = sb("adj_s", [128, N])
        adjt_s = sb("adjt_s", [128, N])
        mask = sb("mask", [128, N])
        ident = sb("ident", [128, 128])
        b0_s, bp_s, gamma_s, lbeta_s = (sb(n, [128, D]) for n in ("b0_s", "bp_s", "gamma_s", "lbeta_s"))
        beta_s = sb("beta_s", [128, 1])
        gb = sb("gb", [128, 5, KB])
        bias_r, bias_z, bias_v = (sb(n, [128, KB]) for n in ("bias_r", "bias_z", "bias_v"))
        minus_half = sb("minus_half", [128, G])
        minus_one = sb("minus_one", [128, G])
        one = sb("one", [128, G])
        eps = sb("eps", [128, G])
        unused = sb("unused", [128, 5])
        wa = sb("wa", [128, KB, 2])

        xin = sb("xin", [128, G, D])
        x1 = sb("x1", [128, G, D])
        chi, clo = pair("c", [128, KB, G, N])
        hs = sb("hs", [128, G, D])
        s12 = sb("s12", [128, G, 2])
        mn = sb("mn", [128, G, D])
        e_s = mn[:, 0:2, :].rearrange("p a (b n) -> p (a b) n", b=2)
        et_s = mn[:, 2:4, :].rearrange("p a (b n) -> p (a b) n", b=2)
        emax, enm, eden, erd = (sb(n, [128, G]) for n in ("emax", "enm", "eden", "erd"))

        x2 = sb("x2", [128, G, D])
        x2b = sb("x2b", [128, G, D])
        fhi, flo = pair("f", [128, KB, G, N])
        k_both = sb("k_both", [128, 2, KB, G, N], F32R)
        khi, klo = k_both[:, 0, :, :, :], k_both[:, 1, :, :, :]
        kd_both = sb("kd_both", [128, 2, KB, HB, 2, N], F32R)
        kd_hi, kd_lo = kd_both[:, 0, :, :, :, :], kd_both[:, 1, :, :, :, :]
        vs = sb("vs", [128, G, D])
        P = [sb(f"p{i}", [128, H, N]) for i in range(2)]
        PT = [sb(f"pt{i}", [128, H, N]) for i in range(2)]
        pmax, pnm, pden, prd = ([sb(f"{n}{i}", [128, H]) for i in range(2)] for n in ("pmax", "pnm", "pden", "prd"))
        ob = sb("ob", [128, G, D])
        on = sb("on", [128, G, D])
        x3 = sb("x3", [128, G, D])

        x3_kept = sb("x3_kept", [128, G, D])
        ht0 = sb("ht0", [128, KB, G, N])
        ht = sb("ht", [128, KB, G, N])
        hhi, hlo = pair("h", [128, KB, G, N])
        ahi, alo = pair("a", [128, KB, G, N])
        hu = sb("hu", [128, KB, G, N])
        rt = sb("rt", [128, KB, G, N])
        zt = sb("zt", [128, KB, G, N])
        rhi, rlo = pair("r", [128, KB, G, N])
        hv = sb("hv", [128, KB, G, N])
        res = hv[:, :, :, :].rearrange("p k g n -> p (k g n)").rearrange("p (g d) -> p g d", g=G)
        hn = sb("hn", [128, G, D])

        def ln_tiles(n):
            return (sb(n + "_bn", [128, G, 6]), sb(n + "_mv", [128, G, 2]), sb(n + "_ve", [128, G]),
                    sb(n + "_rs", [128, G]), sb(n + "_nm", [128, G]), sb(n + "_mr", [128, G]))

        c_ln, m_ln, g_ln = ln_tiles("cln"), ln_tiles("mln"), ln_tiles("gln")

        CP, MP, GP, GQ = (ctx.enter_context(nc.psum_tensor(n, [128, 2, 512], F32)) for n in ("CP", "MP", "GP", "GQ"))

        def feat(ps):
            return ps[:, :, :].rearrange("p k (g n) -> p k g n", g=G)

        def node(ps):
            return ps[:, :, :].rearrange("p a (b d) -> p (a b) d", b=2)

        def by_feat(tile):
            return tile[:, :, :].rearrange("p g (k f) -> p k g f", k=KB)

        def heads(ps):
            return ps[:, :, :].rearrange("p a (h n) -> p (a h) n", h=HB)

        ld_adjt, ld_b0, ld_w0, ld_w1, ld_att, ld_const, ld_gates = (
            sem(n) for n in ("ld_adjt", "ld_b0", "ld_w0", "ld_w1", "ld_att", "ld_const", "ld_gates"))
        pool_consts, k_zeros, wa_done, raw_ready, consts_done = (
            sem(n) for n in ("pool_consts", "k_zeros", "wa_done", "raw_ready", "consts_done"))
        w_hi, w_lo, wa_split, bias_sums = (sem(n) for n in ("w_hi", "w_lo", "wa_split", "bias_sums"))
        x_loaded = sem("x_loaded")
        y_mm, y_hi, y_lo = sem("y_mm"), sem("y_hi"), sem("y_lo")
        out0_mm, x1p = sem("out0_mm"), sem("x1p")
        xb_done = sem("xb_done")
        c_bn, c_stats, c_ve, c_pow, c_nm, c_rstd, c_done = (sem("c_" + n) for n in ("bn", "stats", "ve", "pow", "nm", "rstd", "done"))
        m_bn, m_stats, m_ve, m_pow, m_nm, m_rstd = (sem("m_" + n) for n in ("bn", "stats", "ve", "pow", "nm", "rstd"))
        o_normed, m_done = sem("o_normed"), sem("m_done")
        g_bn, g_stats, g_ve, g_pow, g_nm, g_rstd, g_done = (sem("g_" + n) for n in ("bn", "stats", "ve", "pow", "nm", "rstd", "done"))
        x1t_mm, x1_hi, x1_lo = sem("x1t_mm"), sem("x1_hi"), sem("x1_lo")
        h_mm, h_copied = sem("h_mm"), sem("h_copied")
        s2_mm, e_sum, e_leaky, e_max, e_nm = (sem(n) for n in ("s2_mm", "e_sum", "e_leaky", "e_max", "e_nm"))
        e_exp, e_rden, e_norm = sem("e_exp"), sem("e_rden"), sem("e_norm")
        et_mm, et_copied = sem("et_mm"), sem("et_copied")
        hp_mm = sem("hp_mm")
        el_sum, el_min, el_exp, el_pos, x2p = (sem(n) for n in ("el_sum", "el_min", "el_exp", "el_pos", "x2p"))
        x2t_mm, x2_hi, x2_lo = sem("x2t_mm"), sem("x2_hi"), sem("x2_lo")
        k_mm, k_hi, k_lo, k_spread = sem("k_mm"), sem("k_hi"), sem("k_lo"), sem("k_spread")
        v_mm, v_copied = sem("v_mm"), sem("v_copied")
        q_mm, q_hi, q_lo = sem("q_mm"), sem("q_hi"), sem("q_lo")
        sc_mm, sc_max, sc_nm, sc_exp, sc_rden, sc_norm = (sem(n) for n in ("sc_mm", "sc_max", "sc_nm", "sc_exp", "sc_rden", "sc_norm"))
        pt_mm, pt_copied = sem("pt_mm"), sem("pt_copied")
        o_mm, o_hi, o_lo = sem("o_mm"), sem("o_hi"), sem("o_lo")
        proj_mm, o_biased, on_scaled, res_sum, x3p = (sem(n) for n in ("proj_mm", "o_biased", "on_scaled", "res_sum", "x3p"))
        x2b_done = sem("x2b_done")
        x3_copied, x3t_mm, ht0_set, h0_hi, h0_lo = sem("x3_copied"), sem("x3t_mm"), sem("ht0_set"), sem("h0_hi"), sem("h0_lo")
        a_mm, a_hi, a_lo = sem("a_mm"), sem("a_hi"), sem("a_lo")
        hu_mm, hu_copied = sem("hu_mm"), sem("hu_copied")
        r_mm, r_sum, r_tanh, rh_done, rh_hi, rh_lo = (sem(n) for n in ("r_mm", "r_sum", "r_tanh", "rh_done", "rh_hi", "rh_lo"))
        z_mm, z_sum, z_tanh = sem("z_mm"), sem("z_sum"), sem("z_tanh")
        hv_mm, hv_tanh, hv_diff, hv_scaled, h_new = (sem(n) for n in ("hv_mm", "hv_tanh", "hv_diff", "hv_scaled", "h_new"))
        hn_mm = sem("hn_mm")
        h_hi, h_lo, hn_copied = sem("h_hi"), sem("h_lo"), sem("hn_copied")
        res_done = sem("res_done")
        stored = sem("stored")

        block = ctx.enter_context(nc.Block())

        def later(g):
            return not (isinstance(g, int) and g == 0)

        def two(i):
            return slice(2 * i, 2 * i + 2)

        def scores(g, n):
            return KB * G * g + n

        def block_heads(k_):
            return slice(k_ * HB, k_ * HB + HB)

        def step(g, n):
            return KB * T * g + n

        def inner(g, n):
            return KB * (T - 1) * g + n

        def three(pe, dst, lhs, rhs, start, stop):
            pe.matmul(dst, lhs[0], rhs[1], start=start, stop=False)
            pe.matmul(dst, lhs[1], rhs[0], start=False, stop=False)
            return pe.matmul(dst, lhs[0], rhs[0], start=False, stop=stop)

        def run(order, parts, iterate, prepare={}):
            table = []
            for entry in order.split():
                what, ahead = entry.split("+")
                name, _, k = what.partition(".")
                table.append((parts[name], (int(k),) if k else (), int(ahead), prepare.get(what)))
            most = AHEAD

            def iteration(g):
                for part, k, ahead, ready in table:
                    if not isinstance(g, int) or 0 <= g + ahead < NG:
                        part(g + ahead, *k)
                    if isinstance(g, int) and g + ahead == 0 and ready:
                        ready()

            for g in range(-most, 1):
                iteration(g)
            with iterate(1, NG - most) as g:
                iteration(g)
            for g in range(NG - most, NG):
                iteration(g)

        N_CONST = 10

        def raw(tile, half):
            flat = tile[:, :, :] if len(tile.shape) == 3 else tile[:, :, :, :].rearrange("p k g n -> p (k g) n")
            flat = flat.rearrange("p a b -> p (a b)")
            return flat[:, half * 512:half * 512 + 512].rearrange("p (k n) -> p k n", k=KB)

        raw_w0, raw_w1 = raw(P[0], 0), raw(P[0], 1)
        raw_q, raw_k = raw(P[1], 0), raw(P[1], 1)
        raw_v, raw_p = raw(PT[0], 0), raw(PT[0], 1)
        raw_3 = [raw(PT[1], 0), raw(PT[1], 1)]
        raw_4 = [raw(hu, 0), raw(hu, 1)]
        raw_5 = [raw(rt, 0), raw(rt, 1)]
        raw_u3, raw_u5 = raw(zt, 0), raw(zt, 1)
        a_row = raw(vs, 0)
        WEIGHTS = ((W0, raw_w0), (W1, raw_w1), (WK, raw_k), (WV, raw_v), (WQ, raw_q), (WP, raw_p),
                   (U3, raw_u3), (W4, raw_4[0]), (W3, raw_3[0]), (W5, raw_5[0]), (U5, raw_u5))
        ATT, GATES = slice(2, 6), slice(6, 11)

        @block.sync
        def _(sp):
            def blocks(w):
                return w.rearrange("(k p) n -> p k n", p=128)

            def to_all(v):
                return v.rearrange("(o n) -> o n", o=1).to_broadcast((128, v.shape[0]))

            sp.dma_start(adjt_s[:, :], adj_t).then_inc(ld_adjt, 16)
            sp.dma_start(xin[:, :, :], x[0:G].rearrange("g n d -> n g d")).then_inc(x_loaded, 16)
            sp.dma_start(raw_w0, blocks(w0)).then_inc(ld_w0, 16)
            sp.dma_start(b0_s[:, :], to_all(b0)).then_inc(ld_b0, 16)
            sp.dma_start(raw_w1, blocks(w1)).then_inc(ld_w1, 16)
            for t in range(2):
                sp.dma_start(a_row[:, t, :], to_all(a_vec[t])).then_inc(ld_w1, 16)
            for t, dst in ((1, raw_k), (2, raw_v), (0, raw_q)):
                sp.dma_start(dst, blocks(wqkv[:, t * D:(t + 1) * D])).then_inc(ld_att, 16)
            sp.dma_start(raw_p, blocks(wp)).then_inc(ld_att, 16)
            sp.dma_start(adj_s[:, :], adj).then_inc(ld_const, 16)
            for dst, v in ((beta_s, beta), (bp_s, bp), (gamma_s, gamma), (lbeta_s, lbeta)):
                sp.dma_start(dst[:, :], to_all(v)).then_inc(ld_const, 16)
            for n in range(5):
                sp.dma_start(gb[:, n, :], gate_bias[n]).then_inc(ld_const, 16)
            for w, dst in ((w3, raw_3), (w4, raw_4), (w5, raw_5)):
                for t in range(2):
                    sp.dma_start(dst[t], blocks(w[t * D:(t + 1) * D, :])).then_inc(ld_gates, 16)
            sp.dma_start(raw_u3, blocks(u3)).then_inc(ld_gates, 16)
            sp.dma_start(raw_u5, blocks(u5)).then_inc(ld_gates, 16)

            def load_x(g):
                if later(g):
                    sp.wait_ge(y_mm, KB * g)
                    sp.wait_ge(xb_done, g)
                    sp.dma_start(xin[:, :, :], x[bass.ds(g * G, G)].rearrange("g n d -> n g d")).then_inc(x_loaded, 16)

            def spread_k(g, pair_):
                if pair_ == 0:
                    if later(g):
                        sp.wait_ge(sc_mm, scores(g, 0))
                    else:
                        sp.wait_ge(k_zeros, 1)
                    sp.wait_ge(k_lo, KB * g + KB)
                else:
                    sp.wait_ge(sc_mm, scores(g, 2 * KB))
                own = slice(2 * pair_, 2 * pair_ + 2)
                src = k_both[:, :, :, :, :].rearrange("p s k g n -> p (s k) g n").bitcast(F32)
                dst = kd_both[:, :, :, :, :, :].rearrange("p s k h g n -> p (s k) h g n").bitcast(F32)
                for h in range(HB):
                    r = slice(h * HD, h * HD + HD)
                    sp.dma_start(dst[r, :, h, :, :], src[r, :, own, :]).then_inc(k_spread, 16)

            def store(g):
                sp.wait_ge(g_done, g + 1)
                sp.dma_start(out[bass.ds(g * G, G)].rearrange("g n d -> n g d"), res).then_inc(stored, 16)

            run(SYNC_ORDER, {"c_load": load_x, "m_spread": spread_k, "g_store": store}, sp.Fori)
            sp.wait_ge(stored, 16 * NG)

        @block.gpsimd
        def _(pool):
            pool.memset(ident[:, :], 0.0).then_inc(pool_consts, 1)
            pool.wait_ge(pool_consts, 1)
            pool.affine_select(out=ident[:, :], in_=ident[:, :], compare_op=ALU.not_equal, fill=1.0,
                               base=0, pattern=[[-1, 128]], channel_multiplier=1).then_inc(pool_consts, 1)
            pool.memset(minus_half[:, :], -0.5).then_inc(pool_consts, 1)
            pool.memset(minus_one[:, :], -1.0).then_inc(pool_consts, 1)
            pool.memset(one[:, :], 1.0).then_inc(pool_consts, 1)
            pool.memset(eps[:, :], EPS).then_inc(pool_consts, 1)

            def zeros():
                pool.memset(kd_both[:, :, :, :, :, :].rearrange("p s k h g n -> p (s k h g n)").bitcast(F32), 0.0).then_inc(k_zeros, 1)
                pool.wait_ge(ld_const, 16 * N_CONST)

            def rstd(n, own, tiles, stats, ve, pow_, nm, done):
                _, mv, v, rs, m, mr = tiles
                pool.wait_ge(stats, n + 1)
                pool.tensor_tensor(v[:, own], mv[:, own, 1], eps[:, own], ALU.add).then_inc(ve, 1)
                pool.tensor_tensor(m[:, own], mv[:, own, 0], minus_one[:, own], ALU.mult).then_inc(nm, 1)
                pool.wait_ge(ve, n + 1)
                pool.tensor_tensor(rs[:, own], v[:, own], minus_half[:, own], ALU.pow).then_inc(pow_, 1)
                pool.wait_ge(pow_, n + 1)
                pool.wait_ge(nm, n + 1)
                pool.tensor_tensor(mr[:, own], m[:, own], rs[:, own], ALU.mult).then_inc(done, 1)

            def c_rstd_part(g, n):
                if n >= 2 or later(g):
                    pool.wait_ge(c_done, 4 * g + n - 1)
                rstd(4 * g + n, two(n % 2), c_ln, c_stats, c_ve, c_pow, c_nm, c_rstd)

            def m_rstd_part(g, n):
                if n >= 2:
                    pool.wait_ge(o_normed, 2 * g + n - 1)
                elif later(g):
                    pool.wait_ge(m_done, 2 * g + n - 1)
                rstd(4 * g + n, two(n % 2), m_ln, m_stats, m_ve, m_pow, m_nm, m_rstd)

            def g_rstd_part(g):
                if later(g):
                    pool.wait_ge(g_done, g)
                rstd(g, slice(0, G), g_ln, g_stats, g_ve, g_pow, g_nm, g_rstd)

            def xb(g):
                if not later(g):
                    pool.wait_ge(ld_b0, 16)
                    pool.wait_ge(pool_consts, 6)
                pool.wait_ge(x_loaded, 16 * (g + 1))
                if later(g):
                    pool.wait_ge(x2p, 2 * g)
                pool.tensor_tensor(x1[:, :, :], xin[:, :, :], b0_s[:, :].unsqueeze(1).to_broadcast((128, G, D)),
                                   ALU.add).then_inc(xb_done, 1)

            def e_norm_part(g):
                pool.wait_ge(e_rden, g + 1)
                pool.tensor_tensor(e_s, e_s, erd[:, :].unsqueeze(2).to_broadcast((128, G, N)), ALU.mult).then_inc(e_norm, 1)

            def x2b_part(g):
                pool.wait_ge(c_done, 4 * g + 4)
                if later(g):
                    pool.wait_ge(x3p, 2 * g)
                pool.tensor_tensor(x2b[:, :, :], x2[:, :, :], lbeta_s[:, :].unsqueeze(1).to_broadcast((128, G, D)),
                                   ALU.add).then_inc(x2b_done, 1)

            def p_norm(g, n):
                b, k_ = divmod(n, KB)
                pool.wait_ge(sc_rden, scores(g, n) + 1)
                p = P[b % 2][:, block_heads(k_), :]
                pool.tensor_tensor(p, p, prd[b % 2][:, block_heads(k_)].unsqueeze(2).to_broadcast((128, HB, N)),
                                   ALU.mult).then_inc(sc_norm, 1)

            def residual(g, i):
                own = two(i)
                pool.wait_ge(o_biased, 2 * g + i + 1)
                pool.wait_ge(x2b_done, g + 1)
                pool.tensor_tensor(x2b[:, own, :], ob[:, own, :], x2b[:, own, :], ALU.add).then_inc(res_sum, 1)

            def times_gamma(g, i):
                own = two(i)
                pool.wait_ge(o_normed, 2 * g + i + 1)
                pool.tensor_tensor(on[:, own, :], on[:, own, :], gamma_s[:, :].unsqueeze(1).to_broadcast((128, 2, D)),
                                   ALU.mult).then_inc(on_scaled, 1)

            def keep_x3(g):
                pool.wait_ge(m_done, 2 * g + 2)
                if later(g):
                    pool.wait_ge(res_done, g)
                pool.tensor_tensor(x3_kept[:, :, :], x3[:, :, :], one[:, :].unsqueeze(2).to_broadcast((128, G, D)),
                                   ALU.mult).then_inc(x3_copied, 1)

            run(POOL_ORDER, {"c_xb": xb, "c_rstd": c_rstd_part, "c_enorm": e_norm_part, "m_x2b": x2b_part, "m_pnorm": p_norm,
                             "m_rstd": m_rstd_part, "m_residual": residual, "m_gamma": times_gamma, "m_keep": keep_x3,
                             "g_rstd": g_rstd_part}, pool.Fori, {"c_xb": zeros})

        @block.scalar
        def _(act):
            def normalise(own, dst, src, tiles, rstd, n, done):
                rs, mr = tiles[3], tiles[5]
                act.wait_ge(rstd, n + 1)
                for b in own:
                    last = act.activation(dst[:, b, :], src[:, b, :], ACT.Identity, bias=mr[:, b:b + 1], scale=rs[:, b:b + 1])
                last.then_inc(done, 1)

            def y_hi_part(g, k_):
                act.wait_ge(y_mm, KB * g + k_ + 1)
                if later(g):
                    act.wait_ge(h_mm, G * g)
                act.activation(chi[:, k_, :, :], feat(CP)[:, k_, :, :], ACT.Copy).then_inc(y_hi, 1)

            def x1_norm(g, i):
                normalise((2 * i, 2 * i + 1), x1, x1, c_ln, c_rstd, 4 * g + i, c_done)

            def x1_hi_part(g, k_):
                act.wait_ge(x1t_mm, KB * g + k_ + 1)
                act.activation(chi[:, k_, :, :], feat(CP)[:, k_, :, :], ACT.Copy).then_inc(x1_hi, 1)

            def h_copy(g, b):
                act.wait_ge(h_mm, G * g + b + 1)
                if b == 0 and later(g):
                    act.wait_ge(e_sum, g)
                    act.wait_ge(x2p, 2 * g)
                act.activation(s12[:, b, :], CP[:, b % 2, D:D + 2], ACT.Copy)
                act.activation(hs[:, b, :], CP[:, b % 2, 0:D], ACT.Copy).then_inc(h_copied, 1)

            def e_exp_part(g):
                act.wait_ge(e_nm, g + 1)
                for b in range(G):
                    last = act.activation(e_s[:, b, :], e_s[:, b, :], ACT.Exp, bias=enm[:, b:b + 1],
                                          accum_out=eden[:, b:b + 1])
                last.then_inc(e_exp, 1)

            def et_copy(g):
                act.wait_ge(et_mm, g + 1)
                act.activation(et_s, CP[:, 1, :].rearrange("p (g n) -> p g n", g=G), ACT.Copy).then_inc(et_copied, 1)

            def elu_exp(g, i):
                act.wait_ge(el_min, 2 * g + i + 1)
                act.activation(mn[:, two(i), :], mn[:, two(i), :], ACT.Exp).then_inc(el_exp, 1)

            def x2_norm(g, i):
                if later(g):
                    act.wait_ge(x2t_mm, KB * g)
                    act.wait_ge(x2b_done, g)
                normalise((2 * i, 2 * i + 1), x2, mn, c_ln, c_rstd, 4 * g + 2 + i, c_done)

            def x2_hi_part(g, k_):
                act.wait_ge(x2t_mm, KB * g + k_ + 1)
                if later(g):
                    act.wait_ge(sc_mm, scores(g, 0))
                act.activation(fhi[:, k_, :, :], feat(MP)[:, k_, :, :], ACT.Copy).then_inc(x2_hi, 1)

            def k_hi_part(g, k_):
                act.wait_ge(k_mm, KB * g + k_ + 1)
                if later(g):
                    act.wait_ge(proj_mm, 2 * g)
                act.activation(khi[:, k_, :, :], feat(MP)[:, k_, :, :], ACT.Copy).then_inc(k_hi, 1)

            def v_copy(g, i):
                act.wait_ge(v_mm, 2 * g + i + 1)
                if later(g):
                    act.wait_ge(o_mm, G * g)
                act.activation(vs[:, 2 * i:2 * i + 2, :], node(MP)[:, 2 * i:2 * i + 2, :], ACT.Copy).then_inc(v_copied, 1)

            def q_hi_part(g, k_):
                act.wait_ge(q_mm, KB * g + KB)
                act.activation(fhi[:, k_, :, :], feat(MP)[:, k_, :, :], ACT.Copy).then_inc(q_hi, 1)

            def p_exp(g, n):
                b, k_ = divmod(n, KB)
                act.wait_ge(sc_nm, scores(g, n) + 1)
                p = P[b % 2]
                for h_ in range(k_ * HB, k_ * HB + HB):
                    last = act.activation(p[:, h_, :], p[:, h_, :], ACT.Exp, bias=pnm[b % 2][:, h_:h_ + 1],
                                          scale=SCALE, accum_out=pden[b % 2][:, h_:h_ + 1])
                last.then_inc(sc_exp, 1)

            def pt_copy(g, n):
                b, k_ = divmod(n, KB)
                act.wait_ge(pt_mm, scores(g, n) + 1)
                if b >= 2 or later(g):
                    act.wait_ge(o_mm, G * g + b - 1)
                act.activation(PT[b % 2][:, block_heads(k_), :], heads(MP)[:, block_heads(k_), :], ACT.Copy).then_inc(pt_copied, 1)

            def o_hi_part(g, b):
                act.wait_ge(o_mm, G * g + b + 1)
                if b == 0:
                    act.wait_ge(k_spread, 16 * HB * (2 * g + 2))
                act.activation(khi[:, :, b, :], MP[:, 0, 0:KB * N].rearrange("p (k n) -> p k n", k=KB),
                               ACT.Copy).then_inc(o_hi, 1)

            def o_norm(g, i):
                if later(g):
                    act.wait_ge(m_done, 2 * g)
                normalise((2 * i, 2 * i + 1), on, ob, m_ln, m_rstd, 4 * g + i, o_normed)

            def ht0_part(g):
                act.wait_ge(x3t_mm, g + 1)
                if later(g):
                    act.wait_ge(h_new, step(g - 1, KB))
                act.activation(ht0[:, :, :, :], feat(MP), ACT.Copy).then_inc(ht0_set, 1)

            def h0_hi_part(g):
                act.wait_ge(x3t_mm, g + 1)
                if later(g):
                    act.wait_ge(hu_mm, step(g, 0))
                act.activation(hhi[:, :, :, :], feat(MP), ACT.Copy).then_inc(h0_hi, 1)

            def a_hi_part(g, n):
                k_ = n % KB
                act.wait_ge(a_mm, step(g, n) + 1)
                if n >= KB or later(g):
                    act.wait_ge(z_mm, step(g, n - k_))
                act.activation(ahi[:, k_, :, :], feat(GP)[:, k_, :, :], ACT.Copy).then_inc(a_hi, 1)

            def hu_copy(g, n):
                k_ = n % KB
                act.wait_ge(hu_mm, step(g, n) + 1)
                act.activation(hu[:, k_, :, :], feat(GQ)[:, k_, :, :], ACT.Copy).then_inc(hu_copied, 1)

            def r_tanh_part(g, n):
                k_ = n % KB
                act.wait_ge(r_sum, step(g, n) + 1)
                act.activation(rt[:, k_, :, :], rt[:, k_, :, :], ACT.Tanh, bias=bias_r[:, k_:k_ + 1], scale=0.5).then_inc(r_tanh, 1)

            def rh_hi_part(g, n):
                k_ = n % KB
                act.wait_ge(rh_done, step(g, n) + 1)
                act.activation(rhi[:, k_, :, :], rt[:, k_, :, :], ACT.Copy).then_inc(rh_hi, 1)

            def z_tanh_part(g, n):
                k_ = n % KB
                act.wait_ge(z_sum, step(g, n) + 1)
                act.activation(zt[:, k_, :, :], zt[:, k_, :, :], ACT.Tanh, bias=bias_z[:, k_:k_ + 1], scale=0.5).then_inc(z_tanh, 1)

            def hv_tanh_part(g, n):
                k_ = n % KB
                act.wait_ge(hv_mm, step(g, n) + 1)
                if n < KB and later(g):
                    act.wait_ge(stored, 16 * g)
                act.activation(hv[:, k_, :, :], feat(GP)[:, k_, :, :], ACT.Tanh, bias=bias_v[:, k_:k_ + 1]).then_inc(hv_tanh, 1)

            def h_hi_part(g, n):
                k_ = n % KB
                act.wait_ge(h_new, step(g, n) + 1)
                act.activation(hhi[:, k_, :, :], ht[:, k_, :, :], ACT.Copy).then_inc(h_hi, 1)

            def hn_copy(g, n):
                k_ = n % KB
                act.wait_ge(hn_mm, step(g, n) + 1)
                act.activation(by_feat(hn)[:, k_, :, :], feat(GQ)[:, k_, :, :], ACT.Copy).then_inc(hn_copied, 1)

            def res_norm(g):
                normalise(range(G), res, res, g_ln, g_rstd, g, g_done)

            def split(weights):
                for w, src in weights:
                    act.activation(w[0][:, :, 0:D], src, ACT.Copy).then_inc(w_hi, 1)

            def att_weights():
                act.wait_ge(ld_att, 16 * 4)
                split(WEIGHTS[ATT])

            def gate_weights():
                act.wait_ge(raw_ready, 4)
                split(WEIGHTS[GATES])
                act.wait_ge(consts_done, 4)

            act.wait_ge(ld_w0, 16)
            split(WEIGHTS[0:1])
            act.wait_ge(ld_w1, 16 * 3)
            split(WEIGHTS[1:2])
            run(SCALAR_ORDER, {"c_yhi": y_hi_part, "c_norm0": x1_norm, "c_x1hi": x1_hi_part, "c_hcopy": h_copy,
                               "c_exp": e_exp_part, "c_etcopy": et_copy, "c_eluexp": elu_exp, "c_norm1": x2_norm,
                               "m_x2hi": x2_hi_part, "m_khi": k_hi_part, "m_vcopy": v_copy, "m_qhi": q_hi_part,
                               "m_exp": p_exp, "m_ptcopy": pt_copy, "m_ohi": o_hi_part, "m_norm0": o_norm,
                               "m_ht": ht0_part, "m_h0hi": h0_hi_part, "g_ahi": a_hi_part, "g_hucopy": hu_copy,
                               "g_rtanh": r_tanh_part, "g_rhi": rh_hi_part, "g_ztanh": z_tanh_part,
                               "g_vtanh": hv_tanh_part, "g_hhi": h_hi_part,
                               "g_hncopy": hn_copy, "g_norm": res_norm}, act.Fori,
                {"c_x1hi.1": att_weights, "c_exp": gate_weights})

        @block.vector
        def _(dve):
            def rest(first, weights):
                for n, (w, src) in enumerate(weights):
                    dve.wait_ge(w_hi, first + n + 1)
                    dve.tensor_tensor(w[1][:, :, 0:D], src, w[0][:, :, 0:D], ALU.subtract).then_inc(w_lo, 1)

            def layer1_weights():
                dve.wait_ge(ld_w1, 16 * 3)
                for k_ in range(KB):
                    for t_ in range(2):
                        if k_ or t_:
                            dve.wait_ge(wa_done, 2 * k_ + t_)
                        dve.tensor_tensor_reduce(raw(vs, 1)[:, 0, :], raw_w1[:, k_, :], a_row[:, t_, :], 1.0, 0.0, ALU.mult, ALU.add,
                                                 wa[:, k_, t_:t_ + 1]).then_inc(wa_done, 1)
                rest(1, WEIGHTS[1:2])
                dve.wait_ge(wa_done, 4)
                dve.tensor_copy(W1[0][:, :, D:D + 2], wa[:, :, :]).then_inc(wa_split, 1)
                dve.wait_ge(wa_split, 1)
                dve.tensor_tensor(W1[1][:, :, D:D + 2], wa[:, :, :], W1[0][:, :, D:D + 2], ALU.subtract).then_inc(wa_split, 1)

            def att_weights():
                rest(2, WEIGHTS[ATT])
                dve.wait_ge(ld_const, 16 * N_CONST)
                dve.tensor_scalar(mask[:, :], adj_s[:, :], 0.0, MASKED, ALU.is_equal, ALU.mult).then_inc(consts_done, 1)

            def gate_sums():
                for dst, n1, n2 in ((bias_z, 0, 1), (bias_r, 2, 1), (bias_v, 3, 4)):
                    dve.tensor_tensor(dst[:, :], gb[:, n1, :], gb[:, n2, :], ALU.add).then_inc(bias_sums, 1)
                dve.wait_ge(bias_sums, 3)
                for dst, f in ((bias_z, 0.5), (bias_r, 0.5), (bias_v, 1.0)):
                    dve.tensor_scalar(dst[:, :], dst[:, :], f, None, ALU.mult).then_inc(consts_done, 1)
                dve.wait_ge(ld_gates, 16 * 8)
                for w in (raw_3, raw_4, raw_5):
                    dve.tensor_tensor(w[0], w[0], w[1], ALU.add).then_inc(raw_ready, 1)
                dve.tensor_scalar(raw_u5, raw_u5, 0.5, None, ALU.mult).then_inc(raw_ready, 1)
                dve.wait_ge(raw_ready, 4)

            def gate_weights():
                rest(6, WEIGHTS[GATES])

            rest(0, WEIGHTS[0:1])

            def wait_apart(signal, value, spot):
                dve.wait_ge(signal, value)
                dve.memset(unused[:, spot:spot + 1], 0.0)

            def stats(own, src, tiles, bn, n, done, spot):
                st, mv = tiles[0], tiles[1]
                for b in own:
                    dve.bn_stats(st[:, b, :], src[:, b, :]).then_inc(bn, 1)
                wait_apart(bn, len(own) * (n + 1), spot)
                for b in own:
                    last = dve.bn_aggr(mv[:, b, :], st[:, b, :])
                last.then_inc(done, 1)

            def c_stats_part(g, n):
                i, src = n % 2, (x1 if n < 2 else mn)
                dve.wait_ge(x1p if n < 2 else x2p, 2 * g + i + 1)
                if n >= 2 or later(g):
                    dve.wait_ge(c_rstd, 4 * g + n - 1)
                stats((2 * i, 2 * i + 1), src, c_ln, c_bn, 4 * g + n, c_stats, 0)

            def m_stats_part(g, n):
                i, src = n % 2, (ob if n < 2 else on)
                dve.wait_ge(o_biased if n < 2 else x3p, 2 * g + i + 1)
                if n >= 2 or later(g):
                    dve.wait_ge(m_rstd, 4 * g + n - 1)
                stats((2 * i, 2 * i + 1), src, m_ln, m_bn, 4 * g + n, m_stats, 3)

            def y_lo_part(g, k_):
                dve.wait_ge(y_hi, KB * g + k_ + 1)
                dve.tensor_tensor(clo[:, k_, :, :], feat(CP)[:, k_, :, :], chi[:, k_, :, :], ALU.subtract).then_inc(y_lo, 1)

            def x1_sum(g, i):
                own = two(i)
                dve.wait_ge(out0_mm, 2 * g + i + 1)
                dve.wait_ge(xb_done, g + 1)
                dve.tensor_tensor(x1[:, own, :], node(CP)[:, own, :], x1[:, own, :], ALU.add).then_inc(x1p, 1)

            def x1_lo_part(g, k_):
                dve.wait_ge(x1_hi, KB * g + k_ + 1)
                dve.tensor_tensor(clo[:, k_, :, :], feat(CP)[:, k_, :, :], chi[:, k_, :, :], ALU.subtract).then_inc(x1_lo, 1)

            def scores1(g):
                dve.wait_ge(s2_mm, g + 1)
                if later(g):
                    dve.wait_ge(c_done, 4 * g)
                ps = CP[:, 0, :].rearrange("p (g n) -> p g n", g=G)
                dve.tensor_tensor(e_s, ps, s12[:, :, 0:1].to_broadcast((128, G, N)), ALU.add).then_inc(e_sum, 1)
                dve.wait_ge(e_sum, g + 1)
                dve.scalar_tensor_tensor(out=e_s, in0=e_s, scalar=SLOPE, in1=e_s, op0=ALU.mult, op1=ALU.max).then_inc(e_leaky, 1)
                wait_apart(e_leaky, g + 1, 1)
                for b in range(G):
                    last = dve.tensor_tensor_reduce(e_s[:, b, :], e_s[:, b, :], adj_s[:, :], 1.0, LOWEST, ALU.mult,
                                                    ALU.max, emax[:, b:b + 1])
                last.then_inc(e_max, 1)
                dve.wait_ge(e_max, g + 1)
                dve.tensor_scalar(enm[:, :], emax[:, :], -1.0, None, ALU.mult).then_inc(e_nm, 1)

            def e_reciprocal(g):
                dve.wait_ge(e_exp, g + 1)
                dve.reciprocal(erd[:, :], eden[:, :]).then_inc(e_rden, 1)

            def elu_in(g, i):
                own = two(i)
                dve.wait_ge(hp_mm, 2 * g + i + 1)
                dve.scalar_tensor_tensor(out=hs[:, own, :], in0=hs[:, own, :], scalar=beta_s[:, 0:1], in1=node(CP)[:, own, :],
                                         op0=ALU.mult, op1=ALU.add).then_inc(el_sum, 1)
                dve.wait_ge(el_sum, 2 * g + i + 1)
                dve.tensor_scalar(mn[:, own, :], hs[:, own, :], 0.0, None, ALU.min).then_inc(el_min, 1)

            def elu_out(g, i):
                own = two(i)
                dve.wait_ge(el_exp, 2 * g + i + 1)
                dve.scalar_tensor_tensor(out=hs[:, own, :], in0=hs[:, own, :], scalar=0.0, in1=mn[:, own, :],
                                         op0=ALU.max, op1=ALU.add).then_inc(el_pos, 1)
                dve.wait_ge(el_pos, 2 * g + i + 1)
                dve.scalar_tensor_tensor(out=mn[:, own, :], in0=hs[:, own, :], scalar=-1.0, in1=x1[:, own, :],
                                         op0=ALU.add, op1=ALU.add).then_inc(x2p, 1)

            def x2_lo_part(g, k_):
                dve.wait_ge(x2_hi, KB * g + k_ + 1)
                dve.tensor_tensor(flo[:, k_, :, :], feat(MP)[:, k_, :, :], fhi[:, k_, :, :], ALU.subtract).then_inc(x2_lo, 1)

            def k_lo_part(g, k_):
                dve.wait_ge(k_hi, KB * g + k_ + 1)
                dve.tensor_tensor(klo[:, k_, :, :], feat(MP)[:, k_, :, :], khi[:, k_, :, :], ALU.subtract).then_inc(k_lo, 1)

            def q_lo_part(g, k_):
                dve.wait_ge(q_hi, KB * g + k_ + 1)
                dve.tensor_tensor(flo[:, k_, :, :], feat(MP)[:, k_, :, :], fhi[:, k_, :, :], ALU.subtract).then_inc(q_lo, 1)

            def p_max(g, n):
                b, k_ = divmod(n, KB)
                if b >= 2 or later(g):
                    dve.wait_ge(pt_mm, scores(g, n - 2 * KB) + 1)
                wait_apart(sc_mm, scores(g, n) + 1, 2)
                p = P[b % 2]
                for h_ in range(k_ * HB, k_ * HB + HB):
                    last = dve.tensor_tensor_reduce(p[:, h_, :], heads(MP)[:, h_, :], mask[:, :], 1.0, LOWEST, ALU.add,
                                                    ALU.max, pmax[b % 2][:, h_:h_ + 1])
                last.then_inc(sc_max, 1)
                dve.wait_ge(sc_max, scores(g, n) + 1)
                dve.tensor_scalar(pnm[b % 2][:, block_heads(k_)], pmax[b % 2][:, block_heads(k_)], -SCALE, None,
                                  ALU.mult).then_inc(sc_nm, 1)

            def p_reciprocal(g, n):
                b, k_ = divmod(n, KB)
                dve.wait_ge(sc_exp, scores(g, n) + 1)
                dve.reciprocal(prd[b % 2][:, block_heads(k_)], pden[b % 2][:, block_heads(k_)]).then_inc(sc_rden, 1)

            def o_lo_part(g, b):
                dve.wait_ge(o_hi, G * g + b + 1)
                ps = MP[:, 0, 0:KB * N].rearrange("p (k n) -> p k n", k=KB)
                dve.tensor_tensor(klo[:, :, b, :], ps, khi[:, :, b, :], ALU.subtract).then_inc(o_lo, 1)

            def o_bias(g, i):
                own = two(i)
                dve.wait_ge(proj_mm, 2 * g + i + 1)
                if later(g):
                    dve.wait_ge(res_sum, 2 * g)
                dve.tensor_tensor(ob[:, own, :], node(MP)[:, own, :], bp_s[:, :].unsqueeze(1).to_broadcast((128, 2, D)),
                                  ALU.add).then_inc(o_biased, 1)

            def x3_sum(g, i):
                own = two(i)
                dve.wait_ge(on_scaled, 2 * g + i + 1)
                dve.wait_ge(res_sum, 2 * g + i + 1)
                dve.tensor_tensor(on[:, own, :], x2b[:, own, :], on[:, own, :], ALU.add).then_inc(x3p, 1)

            def x3_norm(g, i):
                dve.wait_ge(m_rstd, 4 * g + 2 + i + 1)
                if later(g):
                    dve.wait_ge(x3_copied, g)
                    dve.wait_ge(x3t_mm, g)
                    dve.wait_ge(a_mm, step(g - 1, KB))
                for b in (2 * i, 2 * i + 1):
                    last = dve.tensor_scalar(x3[:, b, :], on[:, b, :], m_ln[3][:, b:b + 1], m_ln[5][:, b:b + 1],
                                             ALU.mult, ALU.add)
                last.then_inc(m_done, 1)

            def h0_lo_part(g):
                dve.wait_ge(h0_hi, g + 1)
                dve.wait_ge(ht0_set, g + 1)
                dve.tensor_tensor(hlo[:, :, :, :], ht0[:, :, :, :], hhi[:, :, :, :], ALU.subtract).then_inc(h0_lo, 1)

            def a_lo_part(g, n):
                k_ = n % KB
                dve.wait_ge(a_hi, step(g, n) + 1)
                dve.tensor_tensor(alo[:, k_, :, :], feat(GP)[:, k_, :, :], ahi[:, k_, :, :], ALU.subtract).then_inc(a_lo, 1)

            def r_sum_part(g, n):
                k_ = n % KB
                dve.wait_ge(r_mm, step(g, n) + 1)
                dve.wait_ge(hu_copied, step(g, n) + 1)
                dve.tensor_tensor(rt[:, k_, :, :], feat(GP)[:, k_, :, :], hu[:, k_, :, :], ALU.add).then_inc(r_sum, 1)

            def before(n):
                return ht0 if n < KB else ht

            def rh_part(g, n):
                k_ = n % KB
                dve.wait_ge(r_tanh, step(g, n) + 1)
                dve.scalar_tensor_tensor(out=rt[:, k_, :, :], in0=rt[:, k_, :, :], scalar=1.0, in1=before(n)[:, k_, :, :],
                                         op0=ALU.add, op1=ALU.mult).then_inc(rh_done, 1)

            def rh_lo_part(g, n):
                k_ = n % KB
                dve.wait_ge(rh_hi, step(g, n) + 1)
                dve.tensor_tensor(rlo[:, k_, :, :], rt[:, k_, :, :], rhi[:, k_, :, :], ALU.subtract).then_inc(rh_lo, 1)

            def z_sum_part(g, n):
                k_ = n % KB
                dve.wait_ge(z_mm, step(g, n) + 1)
                dve.tensor_tensor(zt[:, k_, :, :], feat(GQ)[:, k_, :, :], hu[:, k_, :, :], ALU.add).then_inc(z_sum, 1)

            def h_update(g, part):
                k_, n = part % KB, step(g, part)
                v_, h_ = hv[:, k_, :, :], before(part)[:, k_, :, :]
                dve.wait_ge(hv_tanh, n + 1)
                dve.tensor_tensor(v_, v_, h_, ALU.subtract).then_inc(hv_diff, 1)
                dve.wait_ge(z_tanh, n + 1)
                dve.wait_ge(hv_diff, n + 1)
                dve.scalar_tensor_tensor(out=v_, in0=zt[:, k_, :, :], scalar=1.0, in1=v_,
                                         op0=ALU.add, op1=ALU.mult).then_inc(hv_scaled, 1)
                dve.wait_ge(hv_scaled, n + 1)
                dve.scalar_tensor_tensor(out=ht[:, k_, :, :], in0=v_, scalar=0.5, in1=h_,
                                         op0=ALU.mult, op1=ALU.add).then_inc(h_new, 1)

            def h_lo_part(g, n):
                k_ = n % KB
                dve.wait_ge(h_hi, inner(g, n) + 1)
                dve.tensor_tensor(hlo[:, k_, :, :], ht[:, k_, :, :], hhi[:, k_, :, :], ALU.subtract).then_inc(h_lo, 1)

            def res_sum_part(g):
                dve.wait_ge(hn_mm, step(g, KB * T))
                dve.wait_ge(x3_copied, g + 1)
                for k_ in range(KB):
                    last = dve.tensor_tensor(by_feat(res)[:, k_, :, :], feat(GQ)[:, k_, :, :], by_feat(x3_kept)[:, k_, :, :], ALU.add)
                last.then_inc(res_done, 1)

            def res_stats(g):
                dve.wait_ge(res_done, g + 1)
                if later(g):
                    dve.wait_ge(g_rstd, g)
                stats(range(G), res, g_ln, g_bn, g, g_stats, 4)

            run(VECTOR_ORDER, {"c_ylo": y_lo_part, "c_x1sum": x1_sum, "c_x1lo": x1_lo_part, "c_scores": scores1,
                               "c_erd": e_reciprocal, "c_eluin": elu_in, "c_eluout": elu_out, "c_stats": c_stats_part,
                               "m_x2lo": x2_lo_part, "m_klo": k_lo_part, "m_qlo": q_lo_part, "m_max": p_max,
                               "m_prd": p_reciprocal, "m_olo": o_lo_part, "m_obias": o_bias, "m_x3sum": x3_sum,
                               "m_stats": m_stats_part, "m_norm1": x3_norm, "m_h0lo": h0_lo_part, "g_alo": a_lo_part,
                               "g_rsum": r_sum_part, "g_rh": rh_part, "g_zsum": z_sum_part,
                               "g_rlo": rh_lo_part, "g_update": h_update, "g_hlo": h_lo_part,
                               "g_res": res_sum_part, "g_stats": res_stats}, dve.Fori,
                {"c_ylo.1": layer1_weights, "c_x1lo.1": att_weights, "c_scores": gate_sums, "c_erd": gate_weights})

        @block.tensor
        def _(pe):
            def features(ps, o, w, hi, lo, start=True, stop=True):
                cols = slice(o * 128, o * 128 + 128)
                for k_ in range(KB):
                    last = three(pe, ps[:, o, :], (w[0][:, k_, cols], w[1][:, k_, cols]),
                                 (flat(hi, k_), flat(lo, k_)), start and k_ == 0, stop and k_ == KB - 1)
                return last

            def flat(tile, k_):
                return tile[:, k_, :, :].rearrange("p g n -> p (g n)")

            def nodes(dst, graphs, w, hi, lo, width=D):
                for b in graphs:
                    for k_ in range(KB):
                        last = three(pe, dst(b), (hi[:, k_, b, :], lo[:, k_, b, :]),
                                     (w[0][:, k_, 0:width], w[1][:, k_, 0:width]), k_ == 0, k_ == KB - 1)
                return last

            def pair_of(ps, i, w, hi, lo):
                return nodes(lambda b: node(ps)[:, b, :], range(2 * i, 2 * i + 2), w, hi, lo)

            def turn_nodes(ps, src, k_):
                for b in range(G):
                    last = pe.transpose(feat(ps)[:, k_, b, :], src[:, b, k_ * 128:k_ * 128 + 128], ident[:, :])
                return last

            def times_adj(ps, src, k_):
                for b in range(G):
                    last = pe.matmul(feat(ps)[:, k_, b, :], src[:, b, k_ * 128:k_ * 128 + 128], adjt_s[:, :],
                                     start=True, stop=True)
                return last

            def y(g, k_):
                if not later(g) and k_ == 0:
                    pe.wait_ge(ld_adjt, 16)
                pe.wait_ge(x_loaded, 16 * (g + 1))
                if later(g):
                    pe.wait_ge(el_sum, 2 * g)
                times_adj(CP, xin, k_).then_inc(y_mm, 1)

            def out0(g, i):
                pe.wait_ge(y_lo, KB * g + KB)
                if not later(g) and i == 0:
                    pe.wait_ge(w_lo, 1)
                pair_of(CP, i, W0, chi, clo).then_inc(out0_mm, 1)

            def x1t(g, k_):
                if not later(g) and k_ == 0:
                    pe.wait_ge(pool_consts, 2)
                pe.wait_ge(c_done, 4 * g + 2)
                turn_nodes(CP, x1, k_).then_inc(x1t_mm, 1)

            def h(g, b):
                if b < 2:
                    pe.wait_ge(x1_lo, KB * g + KB)
                    if not later(g) and b == 0:
                        pe.wait_ge(w_lo, 2)
                        pe.wait_ge(wa_split, 2)
                else:
                    pe.wait_ge(h_copied, G * g + b - 1)
                nodes(lambda b_: CP[:, b_ % 2, 0:D + 2], (b,), W1, chi, clo, D + 2).then_inc(h_mm, 1)

            def s2(g):
                pe.wait_ge(h_copied, G * g + G)
                for b in range(G):
                    last = pe.transpose(CP[:, 0, b * N:b * N + N], s12[:, b, 1:2].to_broadcast((128, 128)), ident[:, :])
                last.then_inc(s2_mm, 1)

            def et(g):
                pe.wait_ge(e_norm, g + 1)
                for b in range(G):
                    last = pe.transpose(CP[:, 1, b * N:b * N + N], e_s[:, b, :], ident[:, :])
                last.then_inc(et_mm, 1)

            def hp(g, i):
                pe.wait_ge(et_copied, g + 1)
                for b in (2 * i, 2 * i + 1):
                    last = pe.matmul(node(CP)[:, b, :], et_s[:, b, :], hs[:, b, :], start=True, stop=True)
                last.then_inc(hp_mm, 1)

            def x2t(g, k_):
                pe.wait_ge(c_done, 4 * g + 4)
                if later(g):
                    pe.wait_ge(ht0_set, g)
                    pe.wait_ge(h0_hi, g)
                turn_nodes(MP, x2, k_).then_inc(x2t_mm, 1)

            def k(g, o):
                if not later(g) and o == 0:
                    pe.wait_ge(w_lo, 6)
                pe.wait_ge(x2_lo, KB * g + KB)
                features(MP, o, WK, fhi, flo).then_inc(k_mm, 1)

            def v(g, i):
                pe.wait_ge(k_lo, KB * g + i + 1)
                pair_of(MP, i, WV, fhi, flo).then_inc(v_mm, 1)

            def q(g, o):
                pe.wait_ge(v_copied, 2 * g + o + 1)
                features(MP, o, WQ, fhi, flo).then_inc(q_mm, 1)

            def score(g, n):
                b, k_ = divmod(n, KB)
                if b == 0:
                    pe.wait_ge(q_lo, KB * g + KB)
                if b == 1:
                    pe.wait_ge(sc_max, scores(g, n - KB) + 1)
                if b % 2 == 0:
                    pe.wait_ge(k_spread, 16 * HB * (2 * g + b // 2 + 1))
                if b >= 2 and k_ == 0:
                    pe.wait_ge(o_lo, G * g + b - 1)
                if b >= 2 and k_ == 1:
                    pe.wait_ge(pt_copied, scores(g, n - 2 * KB) + 1)
                three(pe, MP[:, k_, :], (fhi[:, k_, b, :], flo[:, k_, b, :]),
                      (kd_hi[:, k_, :, b % 2, :], kd_lo[:, k_, :, b % 2, :]), True, True).then_inc(sc_mm, 1)

            def turn(g, n):
                b, k_ = divmod(n, KB)
                pe.wait_ge(sc_norm, scores(g, n) + 1)
                if b < G - 1:
                    pe.wait_ge(sc_max, scores(g, n + KB) + 1)
                elif k_ == 0:
                    pe.wait_ge(o_lo, G * g + b)
                else:
                    pe.wait_ge(pt_copied, scores(g, n - KB) + 1)
                for h_ in range(k_ * HB, k_ * HB + HB):
                    last = pe.transpose(heads(MP)[:, h_, :], P[b % 2][:, h_, :], ident[:, :])
                last.then_inc(pt_mm, 1)

            def mix(g, b):
                pe.wait_ge(pt_copied, scores(g, KB * b + KB))
                for k_ in range(KB):
                    for h_ in range(HB):
                        f = k_ * 128 + h_ * HD
                        last = pe.matmul(MP[h_ * HD:h_ * HD + HD, 0, k_ * N:k_ * N + N],
                                         vs[:, b, f:f + HD], PT[b % 2][:, k_ * HB + h_, :], start=True, stop=True)
                last.then_inc(o_mm, 1)

            def proj(g, i):
                pe.wait_ge(o_lo, G * g + G)
                pair_of(MP, i, WP, khi, klo).then_inc(proj_mm, 1)

            def x3t(g):
                pe.wait_ge(m_done, 2 * g + 2)
                for k_ in range(KB):
                    last = turn_nodes(MP, x3, k_)
                last.then_inc(x3t_mm, 1)

            def a(g, n):
                k_ = n % KB
                if n >= KB:
                    pe.wait_ge(hn_copied, inner(g, n - KB) + 1)
                else:
                    pe.wait_ge(m_done, 2 * g + 2)
                if n >= KB or later(g):
                    pe.wait_ge(hv_tanh, step(g, n - KB) + 1)
                times_adj(GP, x3 if n < KB else hn, k_).then_inc(a_mm, 1)

            def hu_part(g, n):
                o = n % KB
                if n >= KB:
                    pe.wait_ge(h_lo, inner(g, n - o))
                    pe.wait_ge(hn_copied, inner(g, n - KB) + 1)
                else:
                    pe.wait_ge(h0_lo, g + 1)
                    if later(g):
                        pe.wait_ge(res_done, g)
                if not later(g) and n == 0:
                    pe.wait_ge(w_lo, 11)
                features(GQ, o, U3, hhi, hlo).then_inc(hu_mm, 1)

            def r(g, n):
                o = n % KB
                pe.wait_ge(a_lo, step(g, n - o) + KB)
                if not later(g) and n == 0:
                    pe.wait_ge(w_lo, 11)
                features(GP, o, W4, ahi, alo).then_inc(r_mm, 1)

            def z(g, n):
                o = n % KB
                pe.wait_ge(hu_copied, step(g, n) + 1)
                pe.wait_ge(a_lo, step(g, n - o) + KB)
                features(GQ, o, W3, ahi, alo).then_inc(z_mm, 1)

            def v5(g, n):
                pe.wait_ge(r_sum, step(g, n) + 1)
                features(GP, n % KB, W5, ahi, alo, stop=False)

            def u5(g, n):
                o = n % KB
                pe.wait_ge(rh_lo, step(g, n - o) + KB)
                features(GP, o, U5, rhi, rlo, start=False).then_inc(hv_mm, 1)

            def hn_turn(g, n):
                k_ = n % KB
                pe.wait_ge(h_new, step(g, n) + 1)
                pe.wait_ge(z_sum, step(g, n) + 1)
                for b in range(G):
                    last = pe.transpose(feat(GQ)[:, k_, b, :], ht[:, k_, b, :], ident[:, :])
                last.then_inc(hn_mm, 1)

            run(TENSOR_ORDER, {"c_y": y, "c_out0": out0, "c_x1t": x1t, "c_h": h, "c_s2": s2, "c_et": et, "c_hp": hp,
                               "m_x2t": x2t, "m_k": k, "m_v": v, "m_q": q, "m_score": score, "m_turn": turn,
                               "m_mix": mix, "m_proj": proj, "m_x3t": x3t, "g_a": a, "g_hu": hu_part, "g_r": r,
                               "g_z": z, "g_v": v5, "g_u5": u5, "g_turn": hn_turn}, pe.Fori)


def kernel(**inputs):
    import numpy as _np
    import concourse.bacc as _bacc
    from concourse import mybir as _mybir
    from concourse.bass_utils import run_bass_kernel_spmd as _run

    i = {k: _np.asarray(v) for k, v in inputs.items()}

    def by_block(v):
        return v.reshape(KB, 128).T

    arrays = {
        "x": i["x"], "adj": i["adj"], "adj_t": i["adj"].T,
        "w0": i["L0_gnn_weight"], "b0": i["L0_gnn_bias"],
        "w1": i["L1_gnn_W"], "a_vec": i["L1_gnn_a"].reshape(2, D), "beta": i["L1_gnn_beta"],
        "wqkv": i["L2_gnn_w_qkv"], "wp": i["L2_gnn_w_proj"], "bp": i["L2_gnn_b_proj"],
        "gamma": i["L2_gnn_ln_gamma"], "lbeta": i["L2_gnn_ln_beta"],
        "w3": i["L3_gnn_w3_w"].T, "w4": i["L3_gnn_w4_w"].T, "w5": i["L3_gnn_w5_w"].T,
        "u3": i["L3_gnn_u3_w"].T, "u5": i["L3_gnn_u5_w"].T,
        "gate_bias": _np.stack([by_block(i[f"L3_gnn_{n}_b"]) for n in ("w3", "u3", "w4", "w5", "u5")]),
    }
    nc = _bacc.Bacc("TRN2", target_bir_lowering=False, num_devices=1)
    ins, args = {}, []
    for name, a in arrays.items():
        a = _np.ascontiguousarray(a)
        ins[f"in_{name}"] = a
        args.append(nc.dram_tensor(f"in_{name}", a.shape, _mybir.dt.from_np(a.dtype), kind="ExternalInput").ap())
    args.append(nc.dram_tensor("out", (B, N, D), _mybir.dt.float32, kind="ExternalOutput").ap())
    gnn_stack(nc, *args)
    r = _run(nc, [ins], core_ids=[0])
    return r.results[0]["out"]
```
